# Optimizing a Trainium2 kernel written in Bass

```python
import numpy as np
import jax
import jax.numpy as jnp

def _softmax(x, axis=-1):
    return jax.nn.softmax(x, axis=axis)

def _gelu(x):
    return jax.nn.gelu(x, approximate=True)

def _silu(x):
    return jax.nn.silu(x)

def _sigmoid(x):
    return jax.nn.sigmoid(x)

def _layernorm(x, axis=-1, eps=1e-05):
    m = jnp.mean(x, axis=axis, keepdims=True)
    v = jnp.var(x, axis=axis, keepdims=True)
    return (x - m) / jnp.sqrt(v + eps)

def _scatter_add(tgt, idx, src, axis=0):
    return tgt.at[idx].add(src)

def _segment_sum(src, seg, n):
    return jax.ops.segment_sum(src, seg, n)
kernel_name = 'mk_xattn_ffn_d2_seqx_r8_aed9a8'

def setup_inputs(seed: int=0):
    np.random.seed(seed)
    _w = jnp.asarray

    def _rec_inputs():
        import jax
        import jax.numpy as jnp
        _rk = jax.random.key(seed)
        x = -0.0002928 + 1 * jax.random.normal(jax.random.fold_in(_rk, 1), (1, 1024, 128), jnp.float32)
        _lenS = 1024 - jax.random.randint(jax.random.fold_in(_rk, 7), (1,), 0, max(1, 1024 // 4) + 1, jnp.int32)
        _lenS2 = 6404 - jax.random.randint(jax.random.fold_in(_rk, 8), (1,), 0, max(1, 6404 // 4) + 1, jnp.int32)
        _ctx_1024P = jax.random.normal(jax.random.fold_in(_rk, 11), (1, 16, 128), jnp.float32)
        _ctx_1024c = jax.random.dirichlet(jax.random.fold_in(_rk, 511), 0.3 * jnp.ones((16,), jnp.float32), (1, 6404))
        _ctx_1024t = jnp.einsum('bsk,bkd->bsd', _ctx_1024c, _ctx_1024P)
        _ctx_1024t = _ctx_1024t * jax.lax.rsqrt(jnp.mean(jnp.square(_ctx_1024t)) + 1e-12) * 0.953939
        ctx_1024 = 2.81802e-05 + 1.00001 * (_ctx_1024t + 0.3 * jax.random.normal(jax.random.fold_in(_rk, 611), (1, 6404, 128), jnp.float32))
        _validS = jnp.arange(1024)[None, :] < _lenS[:, None]
        _validS2 = jnp.arange(6404)[None, :] < _lenS2[:, None]
        _causal = jnp.tril(jnp.ones((1024, 1024), dtype=bool))
        mask_BxS2_bk0 = jnp.logical_not(jnp.broadcast_to(_validS2[:, :], (1, 6404)))
        return (x, ctx_1024, mask_BxS2_bk0)
    x, ctx_1024, mask_BxS2_bk0 = _rec_inputs()

    def _L0_xattn_setup():
        import jax, jax.numpy as jnp
        import numpy as np
        NUM_HEADS = 16
        key = jax.random.key(seed)
        ks = jax.random.split(key, 7)
        B, Nq, Nkv, D = (4, 128, 512, 128)
        q = jax.random.normal(ks[0], (B, Nq, D), dtype=jnp.float32)
        kv = jax.random.normal(ks[1], (B, Nkv, D), dtype=jnp.float32)
        mask = jax.random.randint(ks[2], (B, Nkv), 0, 2) > 0
        mask = mask.at[:, 0].set(False)
        s = D ** (-0.5)
        Wq = jax.random.normal(ks[3], (D, D), dtype=jnp.float32) * s
        Wkv = jax.random.normal(ks[4], (D, 2 * D), dtype=jnp.float32) * s
        Wproj = jax.random.normal(ks[5], (D, D), dtype=jnp.float32) * s
        bproj = jnp.zeros((D,), dtype=jnp.float32)
        return {'q': q, 'kv': kv, 'key_padding_mask': mask, 'Wq': Wq, 'Wkv': Wkv, 'Wproj': Wproj, 'bproj': bproj}
    _L0_xattn_all = _L0_xattn_setup()
    _L0_xattn_in = {k: v for k, v in _L0_xattn_all.items() if k in ('Wq', 'Wkv', 'Wproj', 'bproj')}
    del _L0_xattn_all

    def _L0_ffn_setup():
        import jax, jax.numpy as jnp
        import numpy as np
        D_MODEL = 128
        N_HEADS = 16
        N_EXPERTS = 8
        TOP_K = 2
        EXPERT_HIDDEN = D_MODEL * 4 // N_EXPERTS

        def layer_norm(x, g, b, eps=1e-05):
            mu = jnp.mean(x, axis=-1, keepdims=True)
            var = jnp.var(x, axis=-1, keepdims=True)
            return (x - mu) * jax.lax.rsqrt(var + eps) * g + b
        key = jax.random.key(seed)
        ks = jax.random.split(key, 12)
        s = 1.0 / np.sqrt(D_MODEL)
        return {'x': jax.random.normal(ks[0], (2, 256, D_MODEL), dtype=jnp.float32), 'Wq': jax.random.normal(ks[1], (D_MODEL, D_MODEL), dtype=jnp.float32) * s, 'Wk': jax.random.normal(ks[2], (D_MODEL, D_MODEL), dtype=jnp.float32) * s, 'Wv': jax.random.normal(ks[3], (D_MODEL, D_MODEL), dtype=jnp.float32) * s, 'Wo': jax.random.normal(ks[4], (D_MODEL, D_MODEL), dtype=jnp.float32) * s, 'g1': jnp.ones((D_MODEL,), jnp.float32), 'b1': jnp.zeros((D_MODEL,), jnp.float32), 'g2': jnp.ones((D_MODEL,), jnp.float32), 'b2': jnp.zeros((D_MODEL,), jnp.float32), 'Wg': jax.random.normal(ks[5], (D_MODEL, N_EXPERTS), dtype=jnp.float32) * s, 'W1': jax.random.normal(ks[6], (N_EXPERTS, D_MODEL, EXPERT_HIDDEN), dtype=jnp.float32) * s, 'W2': jax.random.normal(ks[7], (N_EXPERTS, EXPERT_HIDDEN, D_MODEL), dtype=jnp.float32) * (1.0 / np.sqrt(EXPERT_HIDDEN))}
    _L0_ffn_all = _L0_ffn_setup()
    _L0_ffn_in = {k: v for k, v in _L0_ffn_all.items() if k in ('Wq', 'Wk', 'Wv', 'Wo', 'g1', 'b1', 'g2', 'b2', 'Wg', 'W1', 'W2')}
    del _L0_ffn_all

    def _L1_xattn_setup():
        import jax, jax.numpy as jnp
        import numpy as np
        D_MODEL = 128
        N_HEADS = 16
        HEAD = D_MODEL // N_HEADS
        D_FF = 512
        LN_EPS = 1e-05

        def _layernorm(x, g, b):
            mu = jnp.mean(x, axis=-1, keepdims=True)
            var = jnp.mean(jnp.square(x - mu), axis=-1, keepdims=True)
            return (x - mu) * jax.lax.rsqrt(var + LN_EPS) * g + b

        def _mha(q_in, k_in, v_in, Wq, Wk, Wv, bv, causal):
            q = jnp.einsum('bsd,hde->bhse', q_in, Wq)
            k = jnp.einsum('btd,hde->bhte', k_in, Wk)
            v = jnp.einsum('btd,hde->bhte', v_in, Wv) + bv[None, :, None, :]
            scale = HEAD ** (-0.5)
            scores = jnp.einsum('bhse,bhte->bhst', q, k) * scale
            if causal:
                S, T = (scores.shape[-2], scores.shape[-1])
                mask = jnp.tril(jnp.ones((S, T), dtype=bool))
                scores = jnp.where(mask, scores, -jnp.inf)
            p = jax.nn.softmax(scores, axis=-1)
            o = jnp.einsum('bhst,bhte->bhse', p, v)
            B, H, S, E = o.shape
            return o.transpose(0, 2, 1, 3).reshape(B, S, H * E)
        key = jax.random.key(seed)
        ks = jax.random.split(key, 20)
        B, S, T = (2, 256, 256)
        sd = D_MODEL ** (-0.5)
        inp = {'input_tensor': jax.random.normal(ks[0], (B, S, D_MODEL), jnp.float32), 'encoder_output': jax.random.normal(ks[1], (B, T, D_MODEL), jnp.float32), 'Wq1': jax.random.normal(ks[2], (N_HEADS, D_MODEL, HEAD), jnp.float32) * sd, 'Wk1': jax.random.normal(ks[3], (N_HEADS, D_MODEL, HEAD), jnp.float32) * sd, 'Wv1': jax.random.normal(ks[4], (N_HEADS, D_MODEL, HEAD), jnp.float32) * sd, 'bv1': jnp.zeros((N_HEADS, HEAD), jnp.float32), 'Wq2': jax.random.normal(ks[5], (N_HEADS, D_MODEL, HEAD), jnp.float32) * sd, 'Wk2': jax.random.normal(ks[6], (N_HEADS, D_MODEL, HEAD), jnp.float32) * sd, 'Wv2': jax.random.normal(ks[7], (N_HEADS, D_MODEL, HEAD), jnp.float32) * sd, 'bv2': jnp.zeros((N_HEADS, HEAD), jnp.float32), 'g1': jnp.ones((D_MODEL,), jnp.float32), 'be1': jnp.zeros((D_MODEL,), jnp.float32), 'g2': jnp.ones((D_MODEL,), jnp.float32), 'be2': jnp.zeros((D_MODEL,), jnp.float32), 'g3': jnp.ones((D_MODEL,), jnp.float32), 'be3': jnp.zeros((D_MODEL,), jnp.float32), 'Wf1': jax.random.normal(ks[8], (D_MODEL, D_FF), jnp.float32) * sd, 'bf1': jnp.zeros((D_FF,), jnp.float32), 'Wf2': jax.random.normal(ks[9], (D_FF, D_MODEL), jnp.float32) * D_FF ** (-0.5), 'bf2': jnp.zeros((D_MODEL,), jnp.float32)}
        return inp
    _L1_xattn_all = _L1_xattn_setup()
    _L1_xattn_in = {k: v for k, v in _L1_xattn_all.items() if k in ('Wq1', 'Wk1', 'Wv1', 'bv1', 'Wq2', 'Wk2', 'Wv2', 'bv2', 'g1', 'be1', 'g2', 'be2', 'g3', 'be3', 'Wf1', 'bf1', 'Wf2', 'bf2')}
    del _L1_xattn_all

    def _L1_ffn_setup():
        import jax, jax.numpy as jnp
        import numpy as np
        TOP_K = 2
        NUM_EXPERTS = 8
        key = jax.random.key(seed)
        ks = jax.random.split(key, 8)
        h, d, ds, E = (128, 64, 128, NUM_EXPERTS)
        s = 1.0 / np.sqrt(h)
        return {'x': jax.random.normal(ks[0], (2, 256, h), jnp.float32), 'router': jax.random.normal(ks[1], (h, E), jnp.float32) * s, 'experts_gate': jax.random.normal(ks[2], (E, h, d), jnp.float32) * s, 'experts_up': jax.random.normal(ks[3], (E, h, d), jnp.float32) * s, 'experts_down': jax.random.normal(ks[4], (E, d, h), jnp.float32) * (1.0 / np.sqrt(d)), 'shared_gate': jax.random.normal(ks[5], (h, ds), jnp.float32) * s, 'shared_up': jax.random.normal(ks[6], (h, ds), jnp.float32) * s, 'shared_down': jax.random.normal(ks[7], (ds, h), jnp.float32) * (1.0 / np.sqrt(ds))}
    _L1_ffn_all = _L1_ffn_setup()
    _L1_ffn_in = {k: v for k, v in _L1_ffn_all.items() if k in ('router', 'experts_gate', 'experts_up', 'experts_down', 'shared_gate', 'shared_up', 'shared_down')}
    del _L1_ffn_all
    return {'x': x, 'ctx_1024': ctx_1024, 'mask_BxS2_bk0': mask_BxS2_bk0, 'L0_xattn_Wq': _L0_xattn_in['Wq'], 'L0_xattn_Wkv': _L0_xattn_in['Wkv'], 'L0_xattn_Wproj': _L0_xattn_in['Wproj'], 'L0_xattn_bproj': _L0_xattn_in['bproj'], 'L0_ffn_Wq': _L0_ffn_in['Wq'], 'L0_ffn_Wk': _L0_ffn_in['Wk'], 'L0_ffn_Wv': _L0_ffn_in['Wv'], 'L0_ffn_Wo': _L0_ffn_in['Wo'], 'L0_ffn_g1': _L0_ffn_in['g1'], 'L0_ffn_b1': _L0_ffn_in['b1'], 'L0_ffn_g2': _L0_ffn_in['g2'], 'L0_ffn_b2': _L0_ffn_in['b2'], 'L0_ffn_Wg': _L0_ffn_in['Wg'], 'L0_ffn_W1': _L0_ffn_in['W1'], 'L0_ffn_W2': _L0_ffn_in['W2'], 'L1_xattn_Wq1': _L1_xattn_in['Wq1'], 'L1_xattn_Wk1': _L1_xattn_in['Wk1'], 'L1_xattn_Wv1': _L1_xattn_in['Wv1'], 'L1_xattn_bv1': _L1_xattn_in['bv1'], 'L1_xattn_Wq2': _L1_xattn_in['Wq2'], 'L1_xattn_Wk2': _L1_xattn_in['Wk2'], 'L1_xattn_Wv2': _L1_xattn_in['Wv2'], 'L1_xattn_bv2': _L1_xattn_in['bv2'], 'L1_xattn_g1': _L1_xattn_in['g1'], 'L1_xattn_be1': _L1_xattn_in['be1'], 'L1_xattn_g2': _L1_xattn_in['g2'], 'L1_xattn_be2': _L1_xattn_in['be2'], 'L1_xattn_g3': _L1_xattn_in['g3'], 'L1_xattn_be3': _L1_xattn_in['be3'], 'L1_xattn_Wf1': _L1_xattn_in['Wf1'], 'L1_xattn_bf1': _L1_xattn_in['bf1'], 'L1_xattn_Wf2': _L1_xattn_in['Wf2'], 'L1_xattn_bf2': _L1_xattn_in['bf2'], 'L1_ffn_router': _L1_ffn_in['router'], 'L1_ffn_experts_gate': _L1_ffn_in['experts_gate'], 'L1_ffn_experts_up': _L1_ffn_in['experts_up'], 'L1_ffn_experts_down': _L1_ffn_in['experts_down'], 'L1_ffn_shared_gate': _L1_ffn_in['shared_gate'], 'L1_ffn_shared_up': _L1_ffn_in['shared_up'], 'L1_ffn_shared_down': _L1_ffn_in['shared_down']}

def reference(x, ctx_1024, mask_BxS2_bk0, L0_xattn_Wq, L0_xattn_Wkv, L0_xattn_Wproj, L0_xattn_bproj, L0_ffn_Wq, L0_ffn_Wk, L0_ffn_Wv, L0_ffn_Wo, L0_ffn_g1, L0_ffn_b1, L0_ffn_g2, L0_ffn_b2, L0_ffn_Wg, L0_ffn_W1, L0_ffn_W2, L1_xattn_Wq1, L1_xattn_Wk1, L1_xattn_Wv1, L1_xattn_bv1, L1_xattn_Wq2, L1_xattn_Wk2, L1_xattn_Wv2, L1_xattn_bv2, L1_xattn_g1, L1_xattn_be1, L1_xattn_g2, L1_xattn_be2, L1_xattn_g3, L1_xattn_be3, L1_xattn_Wf1, L1_xattn_bf1, L1_xattn_Wf2, L1_xattn_bf2, L1_ffn_router, L1_ffn_experts_gate, L1_ffn_experts_up, L1_ffn_experts_down, L1_ffn_shared_gate, L1_ffn_shared_up, L1_ffn_shared_down):
    import jax
    import jax.numpy as jnp

    def _L0_xattn_ref(q, kv, key_padding_mask, Wq, Wkv, Wproj, bproj):
        import jax, jax.numpy as jnp
        import numpy as np
        NUM_HEADS = 16
        B, Nq, D = q.shape
        Nkv = kv.shape[1]
        H = NUM_HEADS
        hd = D // H
        scale = hd ** (-0.5)
        qp = (q @ Wq).reshape(B, Nq, H, hd).transpose(0, 2, 1, 3) * scale
        kvp = kv @ Wkv
        k = kvp[..., :D].reshape(B, Nkv, H, hd).transpose(0, 2, 1, 3)
        v = kvp[..., D:].reshape(B, Nkv, H, hd).transpose(0, 2, 1, 3)
        attn = jnp.einsum('bhqd,bhkd->bhqk', qp, k)
        neg_inf = jnp.finfo(attn.dtype).min
        attn = jnp.where(key_padding_mask[:, None, None, :], neg_inf, attn)
        attn = jax.nn.softmax(attn, axis=-1)
        x = jnp.einsum('bhqk,bhkd->bhqd', attn, v)
        x = x.transpose(0, 2, 1, 3).reshape(B, Nq, D)
        return x @ Wproj + bproj

    def _L0_ffn_ref(x, Wq, Wk, Wv, Wo, g1, b1, g2, b2, Wg, W1, W2):
        import jax, jax.numpy as jnp
        import numpy as np
        D_MODEL = 128
        N_HEADS = 16
        N_EXPERTS = 8
        TOP_K = 2
        EXPERT_HIDDEN = D_MODEL * 4 // N_EXPERTS

        def layer_norm(x, g, b, eps=1e-05):
            mu = jnp.mean(x, axis=-1, keepdims=True)
            var = jnp.var(x, axis=-1, keepdims=True)
            return (x - mu) * jax.lax.rsqrt(var + eps) * g + b
        B, S, D = x.shape
        H, dk = (N_HEADS, D // N_HEADS)
        xn = layer_norm(x, g1, b1)
        q = (xn @ Wq).reshape(B, S, H, dk).transpose(0, 2, 1, 3)
        k = (xn @ Wk).reshape(B, S, H, dk).transpose(0, 2, 1, 3)
        v = (xn @ Wv).reshape(B, S, H, dk).transpose(0, 2, 1, 3)
        scores = jnp.einsum('bhqd,bhkd->bhqk', q, k) / np.sqrt(dk)
        attn = jax.nn.softmax(scores, axis=-1)
        o = jnp.einsum('bhqk,bhkd->bhqd', attn, v)
        o = o.transpose(0, 2, 1, 3).reshape(B, S, D) @ Wo
        x = x + o
        xn2 = layer_norm(x, g2, b2)
        xf = xn2.reshape(B * S, D)
        gate = xf @ Wg
        topv, topi = jax.lax.top_k(gate, TOP_K)
        probs = jax.nn.softmax(topv, axis=-1)
        cw = jnp.sum(jax.nn.one_hot(topi, N_EXPERTS, dtype=xf.dtype) * probs[..., None], axis=1)
        h = jax.nn.relu(jnp.einsum('td,edh->teh', xf, W1))
        y = jnp.einsum('teh,ehd->ted', h, W2)
        moe = jnp.einsum('ted,te->td', y, cw).reshape(B, S, D)
        return x + moe

    def _L1_xattn_ref(input_tensor, encoder_output, Wq1, Wk1, Wv1, bv1, Wq2, Wk2, Wv2, bv2, g1, be1, g2, be2, g3, be3, Wf1, bf1, Wf2, bf2):
        import jax, jax.numpy as jnp
        import numpy as np
        D_MODEL = 128
        N_HEADS = 16
        HEAD = D_MODEL // N_HEADS
        D_FF = 512
        LN_EPS = 1e-05

        def _layernorm(x, g, b):
            mu = jnp.mean(x, axis=-1, keepdims=True)
            var = jnp.mean(jnp.square(x - mu), axis=-1, keepdims=True)
            return (x - mu) * jax.lax.rsqrt(var + LN_EPS) * g + b

        def _mha(q_in, k_in, v_in, Wq, Wk, Wv, bv, causal):
            q = jnp.einsum('bsd,hde->bhse', q_in, Wq)
            k = jnp.einsum('btd,hde->bhte', k_in, Wk)
            v = jnp.einsum('btd,hde->bhte', v_in, Wv) + bv[None, :, None, :]
            scale = HEAD ** (-0.5)
            scores = jnp.einsum('bhse,bhte->bhst', q, k) * scale
            if causal:
                S, T = (scores.shape[-2], scores.shape[-1])
                mask = jnp.tril(jnp.ones((S, T), dtype=bool))
                scores = jnp.where(mask, scores, -jnp.inf)
            p = jax.nn.softmax(scores, axis=-1)
            o = jnp.einsum('bhst,bhte->bhse', p, v)
            B, H, S, E = o.shape
            return o.transpose(0, 2, 1, 3).reshape(B, S, H * E)
        x = input_tensor
        sa = _mha(x, x, x, Wq1, Wk1, Wv1, bv1, causal=True)
        x = _layernorm(sa + input_tensor, g1, be1)
        ca = _mha(x, encoder_output, encoder_output, Wq2, Wk2, Wv2, bv2, causal=False)
        x = _layernorm(x + ca, g2, be2)
        ffn = jax.nn.relu(x @ Wf1 + bf1) @ Wf2 + bf2
        x = _layernorm(x + ffn, g3, be3)
        return x

    def _L1_ffn_ref(x, router, experts_gate, experts_up, experts_down, shared_gate, shared_up, shared_down):
        import jax, jax.numpy as jnp
        import numpy as np
        TOP_K = 2
        NUM_EXPERTS = 8
        b, s, h = x.shape
        E = router.shape[1]
        shared_act = jax.nn.silu(jnp.einsum('bsh,hd->bsd', x, shared_gate))
        shared_up_out = jnp.einsum('bsh,hd->bsd', x, shared_up)
        shared_out = jnp.einsum('bsd,dh->bsh', shared_act * shared_up_out, shared_down)
        router_probs = jax.nn.softmax(jnp.einsum('bsh,he->bse', x, router), axis=-1)
        topk_probs, topk_idx = jax.lax.top_k(router_probs, TOP_K)
        coef = jnp.sum(jax.nn.one_hot(topk_idx, E, dtype=x.dtype) * topk_probs[..., None], axis=2)
        coef = coef.reshape(b * s, E)
        x_flat = x.reshape(b * s, h)
        gate = jnp.einsum('th,ehd->etd', x_flat, experts_gate)
        up = jnp.einsum('th,ehd->etd', x_flat, experts_up)
        expert_out = jnp.einsum('etd,edh->eth', jax.nn.silu(gate) * up, experts_down)
        routed = jnp.einsum('eth,te->th', expert_out, coef)
        return routed.reshape(b, s, h) + shared_out
    x = x + _L0_xattn_ref(_layernorm(x, axis=-1), ctx_1024, mask_BxS2_bk0, L0_xattn_Wq, L0_xattn_Wkv, L0_xattn_Wproj, L0_xattn_bproj)
    x = x + _L0_ffn_ref(_layernorm(x, axis=-1), L0_ffn_Wq, L0_ffn_Wk, L0_ffn_Wv, L0_ffn_Wo, L0_ffn_g1, L0_ffn_b1, L0_ffn_g2, L0_ffn_b2, L0_ffn_Wg, L0_ffn_W1, L0_ffn_W2)
    x = x + _L1_xattn_ref(_layernorm(x, axis=-1), ctx_1024, L1_xattn_Wq1, L1_xattn_Wk1, L1_xattn_Wv1, L1_xattn_bv1, L1_xattn_Wq2, L1_xattn_Wk2, L1_xattn_Wv2, L1_xattn_bv2, L1_xattn_g1, L1_xattn_be1, L1_xattn_g2, L1_xattn_be2, L1_xattn_g3, L1_xattn_be3, L1_xattn_Wf1, L1_xattn_bf1, L1_xattn_Wf2, L1_xattn_bf2)
    x = x + _L1_ffn_ref(_layernorm(x, axis=-1), L1_ffn_router, L1_ffn_experts_gate, L1_ffn_experts_up, L1_ffn_experts_down, L1_ffn_shared_gate, L1_ffn_shared_up, L1_ffn_shared_down)
    return x

_drawn_inputs = setup_inputs


def setup_inputs(seed=0):
    import zlib

    import numpy as np

    out = dict(_drawn_inputs(seed))
    spreads = {'L0_xattn_bproj': (0.0, 0.1),
     'L0_ffn_g1': (1.0, 0.2),
     'L0_ffn_b1': (0.0, 0.1),
     'L0_ffn_g2': (1.0, 0.2),
     'L0_ffn_b2': (0.0, 0.1),
     'L1_xattn_bv1': (0.0, 0.3),
     'L1_xattn_bv2': (0.0, 0.298),
     'L1_xattn_g1': (1.0, 0.2),
     'L1_xattn_be1': (0.0, 0.1),
     'L1_xattn_g2': (1.0, 0.2),
     'L1_xattn_be2': (0.0, 0.1),
     'L1_xattn_g3': (1.0, 0.2),
     'L1_xattn_be3': (0.0, 0.1),
     'L1_xattn_bf1': (0.0, 0.371),
     'L1_xattn_bf2': (0.0, 0.279)}
    factors = {}
    for name, (base, spread) in spreads.items():
        noise = np.random.default_rng([zlib.crc32(name.encode()), seed]).standard_normal(out[name].shape)
        drawn = base * np.exp(spread * noise) if base else spread * noise
        out[name] = jnp.asarray(drawn.astype(out[name].dtype))
    for name, factor in factors.items():
        out[name] = (out[name] * factor).astype(out[name].dtype)
    return out
```

```python
from contextlib import ExitStack

import concourse.bass as bass
from concourse import mybir

F32 = mybir.dt.float32
BF16 = mybir.dt.bfloat16
U8 = mybir.dt.uint8
U32 = mybir.dt.uint32
ALU = mybir.AluOpType
ACT = mybir.ActivationFunctionType
AX_X = mybir.AxisListType.X

P = 128
N = 1024
NT = N // P
D = 128
H = 16
E = D // H
BANK = 512
HALVES = N // BANK
TERMS = 6
ROW_MAX = TERMS * E
ROW_MASK = ROW_MAX + 3
BIG = 2.0 ** 127
EPS = 1e-5
NX = 8
DX = 64
CX = NX * DX // P
DMA = 16
VCOLS = 16


def ceil_div(a, b):
    return -(-a // b)


class Attention:
    pass


def attention_plan(name, keys, causal, masked, b_banks, p_slots):
    a = Attention()
    a.name, a.keys, a.causal, a.masked = name, keys, causal, masked
    a.b_banks, a.p_slots = b_banks, p_slots
    a.key_tiles = ceil_div(keys, P)
    wide = 2 * BANK
    if causal:
        a.max_units = [(qt, 0, (qt + 1) * P) for qt in range(NT)]
    else:
        a.max_units = [(qt, k0, min(wide, keys - k0)) for qt in range(NT) for k0 in range(0, keys, wide)]
    a.segments = len(a.max_units) // NT
    a.ring_uses = len(a.max_units) + 1
    a.units = []
    for kt in range(a.key_tiles):
        for half in range(HALVES):
            low = kt * P - half * BANK if causal else 0
            if low < BANK:
                a.units.append((kt, half, 0 if kt < 2 else max(0, low)))
    nb = len(a.units)
    a.batches = [list(range(u, u + 4 if u + 8 <= nb else nb)) for u in range(0, nb - 3, 4)]
    a.batch_of = {u: b for b, units in enumerate(a.batches) for u in units}
    lag = 3
    a.batch_at = [b[-1] + lag for b in a.batches]
    a.batch_at[0] = a.batch_at[1]
    a.tail = [b for b, at in enumerate(a.batch_at) if at >= nb]
    a.evacuate_at = max(a.batch_at[b] - nb for b in a.tail) + 1
    assert (2 * nb) % b_banks == 0 and (2 * nb) % p_slots == 0
    first, last = ceil_div(nb, 12), (nb * 84) // 100
    total = sum(n for _, _, n in a.max_units)
    a.max_at, seen = [], 0
    for _, _, n in a.max_units:
        a.max_at.append(first + (last - first) * seen // total)
        seen += n
    a.turn_at = min(nb - 1, last + max(1, nb // 24))
    return a


def transformer(nc, io, out):
    cross0 = attention_plan("cross0", 6404, causal=False, masked=True, b_banks=3, p_slots=12)
    self0 = attention_plan("self0", N, causal=False, masked=False, b_banks=2, p_slots=16)
    self1 = attention_plan("self1", N, causal=True, masked=False, b_banks=3, p_slots=12)
    cross1 = attention_plan("cross1", 6404, causal=False, masked=False, b_banks=3, p_slots=12)
    attentions = [cross0, self0, self1, cross1]
    S = cross0.keys
    KT = cross0.key_tiles
    FULL = S // P
    REST = S - FULL * P

    with ExitStack() as ctx:
        def sb(name, shape, dt=F32):
            return ctx.enter_context(nc.sbuf_tensor(name, shape, dt))

        def dram(name, shape, dt):
            return nc.dram_tensor(name, shape, dt, kind="Internal").ap()

        sems = {}

        def sem(name):
            if name not in sems:
                sems[name] = ctx.enter_context(nc.semaphore(name))
            return sems[name]

        ps = ctx.enter_context(nc.psum_tensor("ps", [P, 8, BANK], F32))
        A_BANK, B_BANK, ACC_BANK = 0, 4, 7

        x = sb("x", [P, NT, D])
        z = sb("z", [P, NT, D])
        xn = sb("xn", [P, NT, D])
        xT = sb("xT", [P, N])
        attT = sb("attT", [P, N])
        by_key = sb("by_key", [P, KT, D])
        ctxT = sb("ctxT", [P, S])
        k_stage = sb("k_stage", [P, 2, S], BF16)
        q_stage = sb("q_stage", [P, 2, N], BF16)
        v_stage = sb("v_stage", [P, 2, KT, VCOLS])
        probs = sb("probs", [P, 16, BANK])
        acc_out = sb("acc_out", [P, BANK])
        scratch = sb("scratch", [P, 8 * BANK])
        o_parts = scratch[:, 0:4 * BANK].rearrange("p (g q) -> p g q", g=4)
        den_parts = scratch[:, 4 * BANK:8 * BANK].rearrange("p (g q) -> p g q", g=4)
        maxima = sb("maxima", [P, NT, cross0.segments])
        neg_max = sb("neg_max", [P, NT])
        max_rest = sb("max_rest", [P, NT])
        max_parts = sb("max_parts", [P, 3, NT], BF16)
        max_rows = sb("max_rows", [3 * NT, P], BF16)
        whole = scratch[:, 0:2 * BANK].rearrange("p (b n) -> p b n", b=2)
        rest = scratch[:, 2 * BANK:4 * BANK].rearrange("p (b n) -> p b n", b=2)
        parts = scratch[:, 4 * BANK:7 * BANK].bitcast(BF16).rearrange("p (b t n) -> p b t n", b=2, t=3)
        probs_b = probs[:].rearrange("p a b -> p (a b)")
        keep = probs_b[:, 0:S // 2].bitcast(BF16)
        mask_in = probs_b[:, S // 2:S // 2 + S // 4].bitcast(U8)
        drop_row = k_stage[0:1, 0, :]
        hidden = probs_b[:, 0:5 * N].rearrange("p (c n) -> p c n", c=5)
        gated = probs_b[:, 5 * N:5 * N + 2 * 2 * BANK].rearrange("p (s b n) -> p s b n", s=2, b=2)
        stats = sb("stats", [P, NT, 6])
        mean_var = sb("mean_var", [P, NT, 2])
        var_eps = sb("var_eps", [P, NT])
        std = sb("std", [P, NT])
        rstd = sb("rstd", [P, NT])
        logits = sb("logits", [P, NT, NX])
        shifted = sb("shifted", [P, NT, NX])
        row_sum = sb("row_sum", [P, NT])
        top = sb("top", [P, NT, 8])
        top_at = sb("top_at", [P, NT, 8], U32)
        top_atf = sb("top_atf", [P, NT, 2])
        chosen = sb("chosen", [P, 2, NT, NX])
        coef = sb("coef", [P, NT, NX])
        top_w = sb("top_w", [P, 2, NT])
        coefT = sb("coefT", [NX, N])
        ident = sb("ident", [P, P])
        ident_b = sb("ident_b", [P, P], BF16)
        causal_a = sb("causal_a", [P, P], BF16)
        causal_b = sb("causal_b", [P, 2 * P], BF16)
        expert_no = sb("expert_no", [P, NX])
        spread = sb("spread", [NX, CX, P])
        zeros_row = sb("zeros_row", [3, N], BF16)
        ones_row = sb("ones_row", [1, N], BF16)
        W = {}
        loads = []

        def weight(name, shape, source):
            W[name] = sb("w_" + name, shape)
            loads.append((W[name][:], source))

        def row_weight(name, source):
            weight(name, [P, D], source.partition_broadcast(P))

        weight("q_cross0", [P, D], io["L0_xattn_Wq"])
        weight("kv_cross0", [P, 2 * D], io["L0_xattn_Wkv"])
        n_first = len(loads)
        weight("o_cross0", [P, D], io["L0_xattn_Wproj"])
        row_weight("o_bias", io["L0_xattn_bproj"])
        weight("q_self0", [P, D], io["L0_ffn_Wq"])
        weight("k_self0", [P, D], io["L0_ffn_Wk"])
        weight("v_self0", [P, D], io["L0_ffn_Wv"])
        weight("o_self0", [P, D], io["L0_ffn_Wo"])
        for n in ("g1", "b1", "g2", "b2"):
            row_weight("m_" + n, io["L0_ffn_" + n])
        weight("gate0", [P, NX], io["L0_ffn_Wg"])
        weight("up0", [P, NX, DX], io["L0_ffn_W1"].rearrange("e d h -> d e h"))
        weight("down0", [P, CX, D], io["L0_ffn_W2"].rearrange("(c a) h d -> (a h) c d", a=P // DX))
        for n, a in (("1", "self1"), ("2", "cross1")):
            for m in "qkv":
                weight(f"{m}_{a}", [P, H, E], io[f"L1_xattn_W{m}{n}"].rearrange("h d e -> d h e"))
            row_weight("v_bias_" + a, io["L1_xattn_bv" + n].rearrange("h e -> (h e)"))
        for n in ("g1", "be1", "g2", "be2", "g3", "be3"):
            row_weight("d_" + n, io["L1_xattn_" + n])
        weight("f1", [P, 4 * D], io["L1_xattn_Wf1"])
        weight("f1_bias", [P, 4], io["L1_xattn_bf1"].rearrange("(c p) -> p c", p=P))
        weight("f2", [P, 4, D], io["L1_xattn_Wf2"].rearrange("(c p) d -> p c d", p=P))
        row_weight("f2_bias", io["L1_xattn_bf2"])
        weight("router", [P, NX], io["L1_ffn_router"])
        weight("xgate", [P, NX, DX], io["L1_ffn_experts_gate"].rearrange("e d h -> d e h"))
        weight("xup", [P, NX, DX], io["L1_ffn_experts_up"].rearrange("e d h -> d e h"))
        weight("xdown", [P, CX, D], io["L1_ffn_experts_down"].rearrange("(c a) h d -> (a h) c d", a=P // DX))
        weight("sgate", [P, D], io["L1_ffn_shared_gate"])
        weight("sup", [P, D], io["L1_ffn_shared_up"])
        weight("sdown", [P, D], io["L1_ffn_shared_down"])

        def flat(w):
            return w[:] if len(w.shape) == 2 else w[:].rearrange("p a b -> p (a b)")

        for a in attentions:
            a.k_dram = dram("k_" + a.name, [3, P, a.keys], BF16)
            a.q_dram = dram("q_" + a.name, [H, TERMS * E, N], BF16)
            a.o_dram = dram("o_" + a.name, [4, 2, P, BANK], F32)
            a.q_jobs = HALVES
            a.jobs = [("q", c * BANK, BANK) for c in range(HALVES)]
            a.jobs += [("k", c, min(BANK, a.keys - c)) for c in range(0, a.keys, BANK)]
            a.v_banks = [(t, min(4, a.key_tiles - t)) for t in range(0, a.key_tiles, 4)]

        def size(a, kt):
            return min(P, a.keys - kt * P)


        block = ctx.enter_context(nc.Block())

        def head_phases(eng, phase):
            phase(-1, 1, True, False, False)
            phase(0, 0, True, True, False)
            with eng.Fori(0, (H - 2) // 2) as pair:
                phase(pair * 2 + 1, 1, True, True, True)
                phase(pair * 2 + 2, 0, True, True, True)
            phase(H - 1, (H - 1) % 2, False, True, True)

        @block.sync
        def _(sp):
            x_dram = io["x"].rearrange("a (t p) d -> p (a t) d", p=P)
            ctx_dram = io["ctx_1024"].rearrange("a s d -> (a s) d")
            sp.dma_start(x[:], x_dram).then_inc(sem("x_in"), DMA)
            for dst, src in loads[:n_first]:
                sp.dma_start(dst, src).then_inc(sem("first_weights_in"), DMA)
            for t in range(0, FULL, 4):
                n = min(4, FULL - t)
                sp.dma_start(by_key[:, t:t + n, :],
                             ctx_dram[t * P:(t + n) * P, :].rearrange("(t p) d -> p t d", p=P)
                             ).then_inc(sem(f"ctx_in{t // 4}"), DMA)
            sp.dma_start(by_key[0:REST, FULL, :], ctx_dram[FULL * P:S, :]).then_inc(sem("ctx_rest_in"), DMA)

            def load_mask_row():
                sp.wait_ge(sem("stages_cleared"), 2)
                sp.wait_ge(sem("drop_row_ready"), 1)
                for b in range(2):
                    sp.dma_start(k_stage[ROW_MASK:ROW_MASK + 1, b, :], drop_row).then_inc(sem("rows_in"), DMA)
                for b in range(2):
                    sp.dma_start(q_stage[ROW_MASK:ROW_MASK + 1, b, :], ones_row[:]).then_inc(sem("rows_in"), DMA)
                sp.wait_ge(sem("rows_in"), 4 * DMA)

            def clear_mask_row():
                for b in range(2):
                    sp.dma_start(q_stage[ROW_MASK:ROW_MASK + 1, b, :], zeros_row[0:1, :]).then_inc(sem("rows_in"), DMA)
                sp.wait_ge(sem("rows_in"), 6 * DMA)

            def store_parts(a):
                for i, (kind, c0, n) in enumerate(a.jobs):
                    sp.wait_ge(sem(a.name + "_part3"), i + 1)
                    src = parts[:, i % 2]
                    if kind == "k":
                        sp.dma_start(a.k_dram[:, :, c0:c0 + n].rearrange("a p c -> p a c"),
                                     src[:, :, 0:n]).then_inc(sem(a.name + f"_stored{i % 2}"), DMA)
                    else:
                        for term, part in enumerate((0, 0, 0, 1, 1, 2)):
                            sp.dma_start(a.q_dram[:, term * E:(term + 1) * E, c0:c0 + n],
                                         src[:, part, 0:n]).then_inc(sem(a.name + f"_stored{i % 2}"), DMA)
                for par in range(2):
                    n = sum(1 if kind == "k" else TERMS for i, (kind, _, _) in enumerate(a.jobs) if i % 2 == par)
                    sp.wait_ge(sem(a.name + f"_stored{par}"), DMA * n)

            def attention(a):
                nb = len(a.units)

                def stage(h, par):
                    done = sem(a.name + "_staged")
                    rows = bass.ds(h * E, E)
                    sp.dma_start(k_stage[0:3 * E, par, 0:a.keys], a.k_dram[0:3, rows, :]).then_inc(done, DMA)
                    sp.dma_start(k_stage[3 * E:5 * E, par, 0:a.keys], a.k_dram[0:2, rows, :]).then_inc(done, DMA)
                    sp.dma_start(k_stage[5 * E:6 * E, par, 0:a.keys], a.k_dram[0, rows, :]).then_inc(done, DMA)
                    sp.dma_start(q_stage[0:ROW_MAX, par, :], a.q_dram[h]).then_inc(done, DMA)
                    sp.dma_start(q_stage[ROW_MAX:ROW_MASK, par, :], zeros_row[:]).then_inc(done, DMA)

                def put_maxima(h, par):
                    sp.wait_ge(sem(a.name + "_max_read"), (h + 1) * a.ring_uses)
                    sp.dma_start(q_stage[ROW_MAX:ROW_MASK, par, :].rearrange("a (t q) -> a t q", t=NT),
                                 max_rows[:]).then_inc(sem(a.name + "_max_in"), DMA)

                def store_out(h):
                    sp.wait_ge(sem(a.name + "_acc_copied"), h + 1)
                    for g in range(4):
                        sp.dma_start(a.o_dram[g, :, bass.ds(h * E, E), :],
                                     acc_out[32 * g:32 * g + VCOLS, :]).then_inc(sem(a.name + "_acc_free"), DMA)

                def phase(h, par, has_a, has_b, tail):
                    if has_a:
                        if tail:
                            sp.wait_ge(sem(a.name + "_scores"), h * nb)
                        stage(h + 1, 1 - par)
                    if tail:
                        store_out(h - 1)
                    if has_a:
                        put_maxima(h + 1, 1 - par)

                head_phases(sp, phase)
                store_out(H - 1)
                sp.wait_ge(sem(a.name + "_acc_free"), (H + 1) * 4 * DMA)
                sp.dma_start(o_parts, a.o_dram[:, 0].rearrange("g p q -> p g q")).then_inc(sem(a.name + "_out_in"), DMA)
                sp.dma_start(den_parts, a.o_dram[:, 1].rearrange("g p q -> p g q")).then_inc(sem(a.name + "_out_in"), DMA)

            load_mask_row()
            store_parts(cross0)
            for dst, src in loads[n_first:]:
                sp.dma_start(dst, src, allow_slow_non_contiguous=True).then_inc(sem("weights_in"), DMA)
            attention(cross0)
            clear_mask_row()
            for a in attentions[1:]:
                store_parts(a)
                attention(a)
            sp.wait_ge(sem("result_ready"), 1)
            sp.dma_start(out.rearrange("a (t p) d -> p (a t) d", p=P), xn[:]).then_inc(sem("result_out"), DMA)
            sp.wait_ge(sem("result_out"), DMA)

        @block.gpsimd
        def _(pool):
            chain = [0]

            def link(ins):
                chain[0] += 1
                ins.then_inc(sem("pool_chain"), 1)
                pool.wait_ge(sem("pool_chain"), chain[0])

            mask_bytes = io["mask_BxS2_bk0"].rearrange("a s -> (a s)").partition_broadcast(P)
            pool.dma_start(mask_in[:, 0:S], mask_bytes).then_inc(sem("mask_in"), DMA)
            link(nc.gpsimd.memset(ident[:], 0.0))
            nc.gpsimd.affine_select(out=ident[:], in_=ident[:], compare_op=ALU.not_equal, fill=1.0, base=0,
                                    pattern=[[-1, P]], channel_multiplier=1).then_inc(sem("ident_ready"), 1)
            pool.wait_ge(sem("ident_ready"), 1)
            nc.gpsimd.tensor_copy(ident_b[:], ident[:]).then_inc(sem("ident_ready"), 1)
            link(nc.gpsimd.memset(causal_a[:], 0.0))
            nc.gpsimd.affine_select(out=causal_a[:], in_=causal_a[:], compare_op=ALU.is_ge, fill=-BIG, base=0,
                                    pattern=[[-1, P]], channel_multiplier=1).then_inc(sem("masks_ready"), 1)
            link(nc.gpsimd.memset(causal_b[:], 0.0))
            nc.gpsimd.affine_select(out=causal_b[:], in_=causal_b[:], compare_op=ALU.is_ge, fill=-BIG, base=-P,
                                    pattern=[[1, 2 * P]], channel_multiplier=-1).then_inc(sem("masks_ready"), 1)
            for n in range(NX):
                last = nc.gpsimd.memset(expert_no[:, n:n + 1], float(n))
            last.then_inc(sem("expert_consts"), 1)
            link(nc.gpsimd.memset(spread[:], 1.0))
            link(nc.gpsimd.affine_select(out=spread[:], in_=spread[:], compare_op=ALU.is_ge, fill=0.0, base=0,
                                         pattern=[[P, CX], [1, P]], channel_multiplier=-DX))
            nc.gpsimd.affine_select(out=spread[:], in_=spread[:], compare_op=ALU.is_ge, fill=0.0, base=DX - 1,
                                    pattern=[[-P, CX], [-1, P]], channel_multiplier=DX).then_inc(sem("expert_consts"), 1)

            def split(a):
                for i, (kind, c0, n) in enumerate(a.jobs):
                    b = i % 2
                    pool.wait_ge(sem(a.name + "_part1"), i + 1)
                    if i >= 2:
                        pool.wait_ge(sem(a.name + "_part3"), i - 1)
                    nc.gpsimd.tensor_tensor(rest[:, b, 0:n], whole[:, b, 0:n], parts[:, b, 0, 0:n],
                                            ALU.subtract).then_inc(sem(a.name + "_rest"), 1)

            def stage_values(a):
                nav = len(a.batches)

                def stage(h, par):
                    src = by_key[:, :, bass.ds(h * E, E)]
                    full = a.keys // P
                    nc.gpsimd.tensor_copy(v_stage[:, par, 0:full, 0:E],
                                          src[:, 0:full, :]).then_inc(sem(a.name + "_v_staged"), 1)
                    left = a.keys - full * P
                    if left:
                        nc.gpsimd.tensor_copy(v_stage[0:left, par, full, 0:E],
                                              src[0:left, full, :]).then_inc(sem(a.name + "_v_staged"), 1)

                pool.wait_ge(sem(a.name + "_v_ready"), len(a.v_banks))
                stage(0, 0)
                stage(1, 1)
                with pool.Fori(0, (H - 2) // 2) as pair:
                    for par in range(2):
                        h = pair * 2 + 2 + par
                        pool.wait_ge(sem(a.name + "_batches"), (h - 1) * nav)
                        stage(h, par)

            pool.wait_ge(sem("v_cleared"), 1)
            for a in attentions:
                split(a)
                stage_values(a)

        @block.scalar
        def _(act):
            chain = [0]
            count = {"ln": 0, "turn": 0}

            def link(ins):
                chain[0] += 1
                ins.then_inc(sem("act_chain"), 1)
                act.wait_ge(sem("act_chain"), chain[0])

            def layer_norm():
                count["ln"] += 1
                act.wait_ge(sem("ln_variance"), count["ln"])
                nc.scalar.activation(std[:], var_eps[:], ACT.Sqrt).then_inc(sem("ln_std"), 1)

            def turned():
                count["turn"] += 1
                act.wait_ge(sem("turn_psum0"), count["turn"])
                nc.scalar.activation(xT[:, 0:BANK], ps[:, 6, :], ACT.Copy).then_inc(sem("turn_out"), 1)

            def evacuate_ctx(i):
                t, n = cross0.v_banks[i]
                act.wait_ge(sem("ctx_turned"), i + 1)
                w = min(S, (t + n) * P) - t * P
                nc.scalar.activation(ctxT[:, t * P:t * P + w], ps[:, 6 + i % 2, 0:w],
                                     ACT.Copy).then_inc(sem("ctxT_odd"), 1)

            def split(a):
                jobs = a.jobs
                for i in range(len(jobs) + 1):
                    if a is cross0 and i % 2 == 1 and i < len(a.v_banks):
                        evacuate_ctx(i)
                    if i < len(jobs):
                        kind, c0, n = jobs[i]
                        b = i % 2
                        act.wait_ge(sem(a.name + "_whole"), i + 1)
                        if i >= 2:
                            done = sum(1 if k == "k" else TERMS for j, (k, _, _) in enumerate(jobs[:i - 1]) if j % 2 == b)
                            act.wait_ge(sem(a.name + f"_stored{b}"), DMA * done)
                        nc.scalar.activation(parts[:, b, 0, 0:n], whole[:, b, 0:n],
                                             ACT.Copy).then_inc(sem(a.name + "_part1"), 1)
                    if i >= 1:
                        kind, c0, n = jobs[i - 1]
                        b = (i - 1) % 2
                        act.wait_ge(sem(a.name + "_rest"), i)
                        nc.scalar.activation(parts[:, b, 1, 0:n], rest[:, b, 0:n],
                                             ACT.Copy).then_inc(sem(a.name + "_part2"), 1)

            def attention(a):
                nb, nav, done = len(a.units), len(a.batches), sem(a.name + "_probs")

                def evacuate(h):
                    act.wait_ge(sem(a.name + "_batches"), (h + 1) * nav)
                    act.wait_ge(sem(a.name + "_acc_free"), (h + 1) * 4 * DMA)
                    nc.scalar.activation(acc_out[:], ps[:, ACC_BANK, :],
                                         ACT.Copy).then_inc(sem(a.name + "_acc_copied"), 1)

                def phase(h, par, has_a, has_b, tail):
                    if not has_b:
                        return
                    for u, (kt, half, low) in enumerate(a.units):
                        m = size(a, kt)
                        slot = (par * nb + u) % a.p_slots
                        bank = B_BANK + (par * nb + u) % a.b_banks
                        act.wait_ge(sem(a.name + "_scores"), h * nb + u + 1)
                        if u >= a.p_slots:
                            if (u - a.p_slots) % 4 == 0:
                                act.wait_ge(sem(a.name + "_batches"), h * nav + a.batch_of[u - a.p_slots] + 1)
                        elif tail:
                            old = nb + u - a.p_slots
                            if old % 4 == 0 or u == 0:
                                act.wait_ge(sem(a.name + "_batches"), (h - 1) * nav + a.batch_of[old] + 1)
                        nc.scalar.activation(probs[0:m, slot, low:BANK], ps[0:m, bank, low:BANK], ACT.Exp,
                                             scale=float(E) ** -0.5).then_inc(done, 1)
                        if tail and u == a.evacuate_at:
                            evacuate(h - 1)

                head_phases(act, phase)
                evacuate(H - 1)

            layer_norm()
            turned()
            for a in attentions:
                if a is self0 or a is cross1:
                    layer_norm()
                if a is self0 or a is self1:
                    layer_norm()
                if a is not cross0:
                    turned()
                split(a)
                attention(a)
                if a is self0:
                    layer_norm()
                    turned()
                    act.wait_ge(sem("moe0_gap"), 1)
                    nc.scalar.activation(top_w[:, 1, :], top_w[:, 0, :], ACT.Exp).then_inc(sem("moe0_exp"), 1)
                    for u in range(CX * HALVES):
                        act.wait_ge(sem("moe0_up"), u + 1)
                        if u >= 2:
                            act.wait_ge(sem("moe0_hidden"), u - 1)
                        nc.scalar.activation(gated[:, u % 2, 0, :], ps[:, 3 * (u % 2), :],
                                             ACT.Relu).then_inc(sem("moe0_relu"), 1)
                if a is cross1:
                    layer_norm()
                    turned()
                    for u in range(4 * HALVES):
                        c, half = u // HALVES, u % HALVES
                        act.wait_ge(sem("ffn_up"), u + 1)
                        nc.scalar.activation(hidden[:, c, half * BANK:(half + 1) * BANK], ps[:, u % 4, :], ACT.Relu,
                                             bias=W["f1_bias"][:, c:c + 1]).then_inc(sem("ffn_hidden"), 1)
                    layer_norm()
                    layer_norm()
                    turned()
                    act.wait_ge(sem("moe1_shift"), 1)
                    nc.scalar.activation(logits[:], shifted[:], ACT.Exp).then_inc(sem("moe1_exp"), 1)
                    for u in range((CX + 1) * HALVES):
                        act.wait_ge(sem("moe1_up"), u + 1)
                        if u >= 2:
                            act.wait_ge(sem("moe1_hidden"), u - 1)
                        nc.scalar.activation(gated[:, u % 2, 0, :], ps[:, 3 * (u % 2), :],
                                             ACT.Silu).then_inc(sem("moe1_silu"), 1)

        @block.vector
        def _(dve):
            chain = [0]
            count = {"ln": 0, "turn": 0}

            def link(ins):
                chain[0] += 1
                ins.then_inc(sem("dve_chain"), 1)
                dve.wait_ge(sem("dve_chain"), chain[0])

            def tt(out_, a, b, op):
                return nc.vector.tensor_tensor(out_, a, b, op)

            def layer_norm(dst, src, gain=None, bias=None):
                count["ln"] += 1
                for t in range(NT):
                    last = nc.vector.bn_stats(stats[:, t, :], src[:, t, :])
                link(last)
                for t in range(NT):
                    last = nc.vector.bn_aggr(mean_var[:, t, :], stats[:, t, :])
                link(last)
                nc.vector.tensor_scalar(var_eps[:], mean_var[:, :, 1], EPS, None,
                                        ALU.add).then_inc(sem("ln_variance"), 1)
                dve.wait_ge(sem("ln_std"), count["ln"])
                link(nc.vector.reciprocal(rstd[:], std[:]))
                for t in range(NT):
                    last = nc.vector.tensor_scalar(dst[:, t, :], src[:, t, :], mean_var[:, t, 0:1], rstd[:, t:t + 1],
                                                   ALU.subtract, ALU.mult)
                if gain is not None:
                    link(last)
                    link(tt(dst[:], dst[:], W[gain][:].unsqueeze(1).to_broadcast([P, NT, D]), ALU.mult))
                    last = tt(dst[:], dst[:], W[bias][:].unsqueeze(1).to_broadcast([P, NT, D]), ALU.add)
                last.then_inc(sem("ln_out"), 1)
                dve.wait_ge(sem("ln_out"), count["ln"])

            def turned():
                count["turn"] += 1
                dve.wait_ge(sem("turn_psum1"), count["turn"])
                nc.vector.tensor_copy(xT[:, BANK:N], ps[:, 7, :]).then_inc(sem("turn_out"), 1)

            def split(a):
                jobs = a.jobs

                def third(i):
                    _, _, n = jobs[i]
                    dve.wait_ge(sem(a.name + "_part2"), i + 1)
                    tt(parts[:, i % 2, 2, 0:n], rest[:, i % 2, 0:n], parts[:, i % 2, 1, 0:n],
                       ALU.subtract).then_inc(sem(a.name + "_part3"), 1)

                def values(i):
                    t, n = a.v_banks[i]
                    last_is_short = (t + n) * P > a.keys
                    dve.wait_ge(sem(a.name + "_v_psum"), i + 1)
                    src = ps[:, 3 + i % 3, 0:n * D].rearrange("p (t d) -> p t d", t=n)
                    bias = W.get("v_bias_" + a.name)
                    full = n - 1 if last_is_short else n
                    pieces = [(0, full, P)] if full else []
                    if last_is_short:
                        pieces.append((full, n, size(a, t + full)))
                    for lo, hi, m in pieces:
                        dst, s = by_key[0:m, t + lo:t + hi, :], src[0:m, lo:hi, :]
                        if bias is None:
                            last = nc.vector.tensor_copy(dst, s)
                        else:
                            last = tt(dst, s, bias[0:m, :].unsqueeze(1).to_broadcast([m, hi - lo, D]), ALU.add)
                    last.then_inc(sem(a.name + "_v_ready"), 1)

                nv, nj = len(a.v_banks), len(jobs)
                for i in range(max(nj + 2, nv)):
                    if a is cross0 and i % 2 == 0 and i < nv:
                        evacuate_ctx(i)
                    if i < nj:
                        kind, c0, n = jobs[i]
                        dve.wait_ge(sem(a.name + "_psum"), i + 1)
                        if i >= 2:
                            dve.wait_ge(sem(a.name + "_rest"), i - 1)
                            dve.wait_ge(sem(a.name + "_part1"), i - 1)
                        dst, src = whole[:, i % 2, 0:n], ps[:, i % 3, 0:n]
                        if kind == "k" and a.masked:
                            ins = tt(dst, src, keep[:, c0:c0 + n], ALU.mult)
                        else:
                            ins = nc.vector.tensor_copy(dst, src)
                        ins.then_inc(sem(a.name + "_whole"), 1)
                    if 2 <= i < nj + 2:
                        third(i - 2)
                    if i < nv and a is not cross0:
                        values(i)
                    if a is cross0 and 3 <= i < nv + 3:
                        values(i - 3)
                if a is cross0:
                    for i in range(max(nj + 2, nv) - 3, nv):
                        values(i)

            def evacuate_ctx(i):
                t, n = cross0.v_banks[i]
                w = min(S, (t + n) * P) - t * P
                dve.wait_ge(sem("ctx_turned"), i + 1)
                nc.vector.tensor_copy(ctxT[:, t * P:t * P + w], ps[:, 6 + i % 2, 0:w]).then_inc(sem("ctxT_even"), 1)

            def attention(a):
                uses, step = a.ring_uses, sem(a.name + "_max_step")
                STEPS = 5

                def phase(h_now, par_now, has_a, has_b, tail):
                    if not has_a:
                        return
                    h, par = h_now + 1, 1 - par_now
                    for u, (qt, k0, n) in enumerate(a.max_units):
                        b = (par * uses + u) % 2
                        dve.wait_ge(sem(a.name + "_max_scores"), h * uses + u + 1)
                        nc.vector.tensor_reduce(maxima[:, qt, u % a.segments:u % a.segments + 1],
                                                ps[:, A_BANK + 2 * b:A_BANK + 2 * b + 2, :].rearrange(
                                                    "p a b -> p (a b)")[:, 0:n],
                                                AX_X, ALU.max).then_inc(sem(a.name + "_max_read"), 1)
                    dve.wait_ge(sem(a.name + "_max_read"), h * uses + len(a.max_units))

                    def linked(k, ins):
                        ins.then_inc(step, 1)
                        dve.wait_ge(step, h * STEPS + k)

                    linked(1, nc.vector.tensor_reduce(neg_max[:], maxima[:, :, 0:a.segments], AX_X, ALU.max,
                                                      negate=True))
                    linked(2, nc.vector.tensor_copy(max_parts[:, 0, :], neg_max[:]))
                    linked(3, tt(max_rest[:], neg_max[:], max_parts[:, 0, :], ALU.subtract))
                    linked(4, nc.vector.tensor_copy(max_parts[:, 1, :], max_rest[:]))
                    tt(max_parts[:, 2, :], max_rest[:], max_parts[:, 1, :], ALU.subtract).then_inc(step, 1)
                    b = (par * uses + uses - 1) % 2
                    dve.wait_ge(sem(a.name + "_max_scores"), (h + 1) * uses)
                    if has_b:
                        dve.wait_ge(sem(a.name + "_max_in"), h * DMA)
                    nc.vector.tensor_copy(max_rows[:], ps[0:3 * NT, A_BANK + 2 * b, 0:P // 2].bitcast(BF16)
                                          ).then_inc(sem(a.name + "_max_read"), 1)

                head_phases(dve, phase)
                dve.wait_ge(sem(a.name + "_out_in"), 2 * DMA)
                o, den = o_parts, den_parts
                tt(o[:, 0:2, :], o[:, 0:2, :], o[:, 2:4, :], ALU.add)
                link(tt(den[:, 0:2, :], den[:, 0:2, :], den[:, 2:4, :], ALU.add))
                link(nc.vector.reciprocal(den[:, 2:4, :], den[:, 0:2, :]))
                tt(attT[:].rearrange("p (a b) -> p a b", a=2), o[:, 0:2, :], den[:, 2:4, :],
                   ALU.mult).then_inc(sem("attended"), 1)

            def add_result(name, dst, other, bias=None):
                for b in range(2):
                    dve.wait_ge(sem(name), b + 1)
                    ins = tt(dst[:, 4 * b:4 * b + 4, :], ps[:, 6 + b, :].rearrange("p (t d) -> p t d", t=4),
                             other[:, 4 * b:4 * b + 4, :], ALU.add)
                link(ins)
                if bias is not None:
                    link(tt(dst[:], dst[:], W[bias][:].unsqueeze(1).to_broadcast([P, NT, D]), ALU.add))

            def top_two(values):
                for t in range(NT):
                    last = nc.vector.max(top[:, t, :], values[:, t, :])
                link(last)
                for t in range(NT):
                    last = nc.vector.max_index(top_at[:, t, :], top[:, t, :], values[:, t, :])
                link(last)
                link(nc.vector.tensor_copy(top_atf[:], top_at[:, :, 0:2]))
                for k in range(2):
                    last = tt(chosen[:, k], expert_no[:].unsqueeze(1).to_broadcast([P, NT, NX]),
                              top_atf[:, :, k].unsqueeze(2).to_broadcast([P, NT, NX]), ALU.is_equal)
                link(last)

            def weigh(w0, w1):
                tt(chosen[:, 0], chosen[:, 0], w0.unsqueeze(2).to_broadcast([P, NT, NX]), ALU.mult)
                link(tt(chosen[:, 1], chosen[:, 1], w1.unsqueeze(2).to_broadcast([P, NT, NX]), ALU.mult))
                tt(coef[:], chosen[:, 0], chosen[:, 1], ALU.add).then_inc(sem("coef_ready"), 1)

            def coef_turned(k):
                for b in range(2):
                    dve.wait_ge(sem("coef_psum"), 2 * k + b + 1)
                    nc.vector.tensor_copy(coefT[:, b * BANK:(b + 1) * BANK],
                                          ps[0:NX, 6 + b, :]).then_inc(sem("coefT_ready"), 1)

            nc.vector.memset(ps[:, ACC_BANK, :], 0.0).then_inc(sem("acc_cleared"), 1)
            for i, a in reversed(list(enumerate(attentions))):
                nc.vector.memset(acc_out[:, i * P:(i + 1) * P], 0.0).then_inc(sem(a.name + "_acc_free"), 4 * DMA)
            nc.vector.memset(ones_row[:], 1.0)
            nc.vector.memset(zeros_row[:], 0.0)
            nc.vector.memset(q_stage[:], 0.0).then_inc(sem("stages_cleared"), 1)
            dve.wait_ge(sem("x_in"), DMA)
            layer_norm(xn, x)
            turned()
            dve.wait_ge(sem("mask_in"), DMA)
            link(nc.vector.tensor_scalar(keep, mask_in[:, 0:S], -1.0, 1.0, ALU.mult, ALU.add))
            nc.vector.memset(k_stage[32:64, :, :], 1.0)
            nc.vector.memset(k_stage[64:P, :, :], 0.0).then_inc(sem("stages_cleared"), 1)
            nc.vector.tensor_scalar(drop_row, keep[0:1, :], BIG, -BIG, ALU.mult, ALU.add
                                    ).then_inc(sem("drop_row_ready"), 1)
            nc.vector.memset(v_stage[:], 1.0).then_inc(sem("v_cleared"), 1)

            split(cross0)
            attention(cross0)
            add_result("cross0_result", x, x, "o_bias")

            layer_norm(z, x)
            layer_norm(xn, z, "m_g1", "m_b1")
            turned()
            split(self0)
            attention(self0)
            add_result("self0_result", z, z)
            layer_norm(xn, z, "m_g2", "m_b2")
            turned()
            dve.wait_ge(sem("gate_logits"), 1)
            link(nc.vector.tensor_copy(logits[:].rearrange("p t e -> p (t e)"), ps[:, 5, 0:NT * NX]))
            top_two(logits)
            tt(top_w[:, 0, :], top[:, :, 1], top[:, :, 0], ALU.subtract).then_inc(sem("moe0_gap"), 1)
            dve.wait_ge(sem("moe0_exp"), 1)
            link(nc.vector.tensor_scalar(row_sum[:], top_w[:, 1, :], 1.0, None, ALU.add))
            link(nc.vector.reciprocal(top_w[:, 0, :], row_sum[:]))
            link(tt(top_w[:, 1, :], top_w[:, 1, :], top_w[:, 0, :], ALU.mult))
            weigh(top_w[:, 0, :], top_w[:, 1, :])
            coef_turned(0)
            for u in range(CX * HALVES):
                c, half = u // HALVES, u % HALVES
                dve.wait_ge(sem("moe0_relu"), u + 1)
                tt(hidden[:, c, half * BANK:(half + 1) * BANK], ps[:, 3 * (u % 2) + 1, :], gated[:, u % 2, 0, :],
                   ALU.mult).then_inc(sem("moe0_hidden"), 1)
            add_result("moe0_result", z, z)
            link(tt(x[:], x[:], z[:], ALU.add))

            layer_norm(z, x)
            turned()
            split(self1)
            attention(self1)
            add_result("self1_result", z, z)
            layer_norm(z, z, "d_g1", "d_be1")
            turned()
            split(cross1)
            attention(cross1)
            add_result("cross1_result", z, z)
            layer_norm(z, z, "d_g2", "d_be2")
            turned()
            add_result("ffn_result", z, z, "f2_bias")
            layer_norm(z, z, "d_g3", "d_be3")
            link(tt(x[:], x[:], z[:], ALU.add))

            layer_norm(z, x)
            turned()
            dve.wait_ge(sem("gate_logits"), 2)
            link(nc.vector.tensor_copy(logits[:].rearrange("p t e -> p (t e)"), ps[:, 5, 0:NT * NX]))
            link(nc.vector.tensor_reduce(row_sum[:], logits[:], AX_X, ALU.max))
            tt(shifted[:], logits[:], row_sum[:].unsqueeze(2).to_broadcast([P, NT, NX]),
               ALU.subtract).then_inc(sem("moe1_shift"), 1)
            dve.wait_ge(sem("moe1_exp"), 1)
            link(nc.vector.tensor_reduce(row_sum[:], logits[:], AX_X, ALU.add))
            link(nc.vector.reciprocal(top_w[:, 0, :], row_sum[:]))
            link(tt(logits[:], logits[:], top_w[:, 0, :].unsqueeze(2).to_broadcast([P, NT, NX]), ALU.mult))
            top_two(logits)
            weigh(top[:, :, 0], top[:, :, 1])
            coef_turned(1)
            for u in range((CX + 1) * HALVES):
                c, half = u // HALVES, u % HALVES
                dst = hidden[:, c, half * BANK:(half + 1) * BANK]
                dve.wait_ge(sem("moe1_silu"), u + 1)
                first = 3 * (u % 2)
                if c < CX:
                    link(tt(gated[:, u % 2, 1, :], ps[:, first + 1, :], gated[:, u % 2, 0, :], ALU.mult))
                    ins = tt(dst, ps[:, first + 2, :], gated[:, u % 2, 1, :], ALU.mult)
                else:
                    ins = tt(dst, ps[:, first + 1, :], gated[:, u % 2, 0, :], ALU.mult)
                ins.then_inc(sem("moe1_hidden"), 1)
            for b in range(2):
                dve.wait_ge(sem("moe1_result"), b + 1)
                ins = tt(xn[:, 4 * b:4 * b + 4, :], ps[:, 6 + b, :].rearrange("p (t d) -> p t d", t=4),
                         x[:, 4 * b:4 * b + 4, :], ALU.add)
            ins.then_inc(sem("result_ready"), 1)

        @block.tensor
        def _(pe):
            count = {"turn": 0}

            def mm(out_, lhsT, rhs, start=True, stop=True):
                return nc.tensor.matmul(out_, lhsT, rhs, start=start, stop=stop)

            def turn(src, ln):
                count["turn"] += 1
                pe.wait_ge(sem("ln_out"), ln)
                for b in range(2):
                    for t in range(4):
                        last = nc.tensor.transpose(ps[:, 6 + b, t * P:(t + 1) * P], src[:, 4 * b + t, :], ident[:])
                    last.then_inc(sem(f"turn_psum{b}"), 1)
                pe.wait_ge(sem("turn_out"), 2 * count["turn"])

            def project(a, w_q, w_k, w_v, kT, before=None):
                nj, nv = len(a.jobs), len(a.v_banks)
                for i in range(max(nj, nv)):
                    if before:
                        before(i)
                    if i < nj:
                        kind, c0, n = a.jobs[i]
                        if i >= 3:
                            pe.wait_ge(sem(a.name + "_whole"), i - 2)
                        src, w = (xT, w_q) if kind == "q" else (kT, w_k)
                        mm(ps[:, i % 3, 0:n], w, src[:, c0:c0 + n]).then_inc(sem(a.name + "_psum"), 1)
                    if i < nv:
                        t, n = a.v_banks[i]
                        if i >= 3:
                            pe.wait_ge(sem(a.name + "_v_ready"), i - 2)
                        for j in range(n):
                            m = size(a, t + j)
                            last = mm(ps[0:m, 3 + i % 3, j * D:(j + 1) * D], kT[:, (t + j) * P:(t + j) * P + m], w_v)
                        last.then_inc(sem(a.name + "_v_psum"), 1)

            def attention(a):
                nb, uses, nav = len(a.units), a.ring_uses, len(a.batches)
                last_unit = {}
                for u, (kt, half, low) in enumerate(a.units):
                    last_unit[(kt % 2, half)] = u

                def pass_a(h, par, u, early):
                    qt, k0, n = a.max_units[u]
                    b = (par * uses + u) % 2
                    if u == 0:
                        pe.wait_ge(sem(a.name + "_staged"), (h + 1) * 5 * DMA)
                    if not (early and u < 2):
                        pe.wait_ge(sem(a.name + "_max_read"), h * uses + u - 1)
                    q = q_stage[:, par, qt * P:(qt + 1) * P]
                    for c in range(0, n, BANK):
                        w = min(BANK, n - c)
                        diag = a.causal and c + w == n
                        last = mm(ps[:, A_BANK + 2 * b + c // BANK, 0:w], q, k_stage[:, par, k0 + c:k0 + c + w],
                                  stop=not diag)
                        if diag:
                            last = mm(ps[:, A_BANK + 2 * b + c // BANK, w - P:w], ident_b[:], causal_a[:],
                                      start=False)
                    last.then_inc(sem(a.name + "_max_scores"), 1)

                def turn_maxima(h, par):
                    b = (par * uses + uses - 1) % 2
                    pe.wait_ge(sem(a.name + "_max_step"), (h + 1) * 5)
                    pe.wait_ge(sem(a.name + "_max_read"), (h + 1) * uses - 2)
                    nc.tensor.transpose(ps[0:3 * NT, A_BANK + 2 * b, 0:P // 2].bitcast(BF16),
                                        max_parts[:].rearrange("p a t -> p (a t)"),
                                        ident_b[:]).then_inc(sem(a.name + "_max_scores"), 1)

                def pass_b(h, par, u, early):
                    kt, half, low = a.units[u]
                    m = size(a, kt)
                    bank = B_BANK + (par * nb + u) % a.b_banks
                    if u == 0:
                        pe.wait_ge(sem(a.name + "_max_in"), (h + 1) * DMA)
                    if not (early and u < a.b_banks):
                        pe.wait_ge(sem(a.name + "_probs"), h * nb + u + 1 - a.b_banks)
                    diag = a.causal and kt // 4 == half
                    last = mm(ps[0:m, bank, low:BANK], k_stage[:, par, kt * P:kt * P + m],
                              q_stage[:, par, half * BANK + low:(half + 1) * BANK], stop=not diag)
                    if diag:
                        hi = (kt % 4 + 1) * P
                        last = mm(ps[:, bank, low:hi], ident_b[:], causal_b[:, 2 * P - (hi - low):2 * P],
                                  start=False)
                    last.then_inc(sem(a.name + "_scores"), 1)

                def values(h, par, b):
                    units = a.batches[b]
                    pe.wait_ge(sem(a.name + "_probs"), h * nb + units[-1] + 1)
                    if b == 0:
                        pe.wait_ge(sem(a.name + "_v_staged"), (h + 1) * (1 if a.keys % P == 0 else 2))
                        if not (isinstance(h, int) and h == 0):
                            pe.wait_ge(sem(a.name + "_acc_copied"), h)
                    for u in units:
                        kt, half, low = a.units[u]
                        m = size(a, kt)
                        g = (kt % 2) * 2 + half
                        last = mm(ps[32 * g:32 * g + VCOLS, ACC_BANK, low:BANK], v_stage[0:m, par, kt, :],
                                  probs[0:m, (par * nb + u) % a.p_slots, low:BANK],
                                  start=kt < 2, stop=u == last_unit[(kt % 2, half)])
                    last.then_inc(sem(a.name + "_batches"), 1)

                def phase(h, par, has_a, has_b, tail):
                    if not has_b:
                        for u in range(len(a.max_units)):
                            pass_a(h + 1, 1 - par, u, True)
                        turn_maxima(h + 1, 1 - par)
                        return
                    for u in range(nb):
                        pass_b(h, par, u, not tail)
                        if tail:
                            for b in a.tail:
                                if a.batch_at[b] - nb == u:
                                    values(h - 1, 1 - par, b)
                        for b in range(nav):
                            if a.batch_at[b] == u:
                                values(h, par, b)
                        if has_a:
                            for v, at in enumerate(a.max_at):
                                if at == u:
                                    pass_a(h + 1, 1 - par, v, False)
                            if a.turn_at == u:
                                turn_maxima(h + 1, 1 - par)

                head_phases(pe, phase)
                for b in a.tail:
                    values(H - 1, (H - 1) % 2, b)

            def out_tiles(name, pairs):
                for b in range(2):
                    for t in range(4 * b, 4 * b + 4):
                        for i, (lhs, rhs) in enumerate(pairs):
                            last = mm(ps[:, 6 + b, (t % 4) * D:(t % 4 + 1) * D], lhs[:, t * P:(t + 1) * P], rhs,
                                      start=i == 0, stop=i == len(pairs) - 1)
                    last.then_inc(sem(name), 1)

            def turn_back(name):
                for b in range(2):
                    for t in range(4):
                        last = nc.tensor.transpose(ps[:, 6 + b, t * P:(t + 1) * P],
                                                   attT[:, (4 * b + t) * P:(4 * b + t + 1) * P], ident[:])
                    last.then_inc(sem(name), 1)

            def gate(w):
                for t in range(NT):
                    last = mm(ps[:, 5, t * NX:(t + 1) * NX], xT[:, t * P:(t + 1) * P], w)
                last.then_inc(sem("gate_logits"), 1)

            def turn_coef(k):
                pe.wait_ge(sem("coef_ready"), k + 1)
                for b in range(2):
                    for t in range(4):
                        last = nc.tensor.transpose(ps[0:NX, 6 + b, t * P:(t + 1) * P], coef[:, 4 * b + t, :], ident[:])
                    last.then_inc(sem("coef_psum"), 1)
                pe.wait_ge(sem("coefT_ready"), 2 * (k + 1))

            pe.wait_ge(sem("ident_ready"), 2)
            pe.wait_ge(sem("acc_cleared"), 1)
            turn(xn, 1)
            pe.wait_ge(sem("first_weights_in"), DMA * n_first)

            def turn_context(i):
                t, n = cross0.v_banks[i]
                if i >= 2:
                    pe.wait_ge(sem("ctxT_odd" if i % 2 else "ctxT_even"), i // 2)
                for j in range(n):
                    m = size(cross0, t + j)
                    if (t + j) % 4 == 0 and m == P:
                        pe.wait_ge(sem(f"ctx_in{(t + j) // 4}"), DMA)
                    if m < P:
                        pe.wait_ge(sem("ctx_rest_in"), DMA)
                    last = nc.tensor.transpose(ps[:, 6 + i % 2, j * P:j * P + m], by_key[0:m, t + j, :],
                                               ident[0:m, 0:m])
                last.then_inc(sem("ctx_turned"), 1)

            def context_first(i):
                for b in ([0, 1] if i == 0 else [i + 1]):
                    if b < len(cross0.v_banks):
                        turn_context(b)

            def cross0_before(i):
                context_first(i)
                need = min(i, len(cross0.v_banks) - 1)
                pe.wait_ge(sem("ctxT_even"), need // 2 + 1)
                if need >= 1:
                    pe.wait_ge(sem("ctxT_odd"), (need + 1) // 2)

            kv = W["kv_cross0"]
            project(cross0, W["q_cross0"][:], kv[:, 0:D], kv[:, D:2 * D], ctxT, before=cross0_before)
            pe.wait_ge(sem("rows_in"), 4 * DMA)
            attention(cross0)
            pe.wait_ge(sem("attended"), 1)
            pe.wait_ge(sem("weights_in"), DMA * (len(loads) - n_first))
            out_tiles("cross0_result", [(attT, W["o_cross0"][:])])

            turn(xn, 3)
            project(self0, W["q_self0"][:], W["k_self0"][:], W["v_self0"][:], xT)
            pe.wait_ge(sem("rows_in"), 6 * DMA)
            attention(self0)
            pe.wait_ge(sem("attended"), 2)
            out_tiles("self0_result", [(attT, W["o_self0"][:])])
            turn(xn, 4)
            gate(W["gate0"][:])
            pe.wait_ge(sem("expert_consts"), 2)
            turn_coef(0)
            for u in range(CX * HALVES):
                c, half = u // HALVES, u % HALVES
                if u >= 2:
                    pe.wait_ge(sem("moe0_hidden"), u - 1)
                cols = slice(half * BANK, (half + 1) * BANK)
                mm(ps[:, 3 * (u % 2) + 1, :], spread[:, c, :], coefT[:, cols])
                mm(ps[:, 3 * (u % 2), :], flat(W["up0"])[:, c * P:(c + 1) * P], xT[:, cols]).then_inc(sem("moe0_up"), 1)
            pe.wait_ge(sem("moe0_hidden"), CX * HALVES)
            out_tiles("moe0_result", [(hidden[:, c, :], W["down0"][:, c, :]) for c in range(CX)])

            turn(z, 5)
            pe.wait_ge(sem("masks_ready"), 2)
            project(self1, flat(W["q_self1"]), flat(W["k_self1"]), flat(W["v_self1"]), xT)
            attention(self1)
            pe.wait_ge(sem("attended"), 3)
            turn_back("self1_result")
            turn(z, 6)
            project(cross1, flat(W["q_cross1"]), flat(W["k_cross1"]), flat(W["v_cross1"]), ctxT)
            attention(cross1)
            pe.wait_ge(sem("attended"), 4)
            turn_back("cross1_result")
            turn(z, 7)
            for u in range(4 * HALVES):
                c, half = u // HALVES, u % HALVES
                if u >= 4:
                    pe.wait_ge(sem("ffn_hidden"), u - 3)
                mm(ps[:, u % 4, :], W["f1"][:, c * P:(c + 1) * P],
                   xT[:, half * BANK:(half + 1) * BANK]).then_inc(sem("ffn_up"), 1)
            pe.wait_ge(sem("ffn_hidden"), 4 * HALVES)
            out_tiles("ffn_result", [(hidden[:, c, :], W["f2"][:, c, :]) for c in range(4)])
            turn(z, 9)
            gate(W["router"][:])
            turn_coef(1)
            for u in range((CX + 1) * HALVES):
                c, half = u // HALVES, u % HALVES
                if u >= 2:
                    pe.wait_ge(sem("moe1_hidden"), u - 1)
                cols = slice(half * BANK, (half + 1) * BANK)
                first = 3 * (u % 2)
                if c < CX:
                    mm(ps[:, first + 2, :], spread[:, c, :], coefT[:, cols])
                    w_up, w_gate = (flat(W[n])[:, c * P:(c + 1) * P] for n in ("xup", "xgate"))
                else:
                    w_up, w_gate = W["sup"][:], W["sgate"][:]
                mm(ps[:, first + 1, :], w_up, xT[:, cols])
                mm(ps[:, first, :], w_gate, xT[:, cols]).then_inc(sem("moe1_up"), 1)
            pe.wait_ge(sem("moe1_hidden"), (CX + 1) * HALVES)
            out_tiles("moe1_result", [(hidden[:, c, :], W["xdown"][:, c, :]) for c in range(CX)]
                      + [(hidden[:, CX, :], W["sdown"][:])])


_INS = ['x', 'ctx_1024', 'mask_BxS2_bk0', 'L0_xattn_Wq', 'L0_xattn_Wkv', 'L0_xattn_Wproj', 'L0_xattn_bproj',
        'L0_ffn_Wq', 'L0_ffn_Wk', 'L0_ffn_Wv', 'L0_ffn_Wo', 'L0_ffn_g1', 'L0_ffn_b1', 'L0_ffn_g2', 'L0_ffn_b2',
        'L0_ffn_Wg', 'L0_ffn_W1', 'L0_ffn_W2', 'L1_xattn_Wq1', 'L1_xattn_Wk1', 'L1_xattn_Wv1', 'L1_xattn_bv1',
        'L1_xattn_Wq2', 'L1_xattn_Wk2', 'L1_xattn_Wv2', 'L1_xattn_bv2', 'L1_xattn_g1', 'L1_xattn_be1',
        'L1_xattn_g2', 'L1_xattn_be2', 'L1_xattn_g3', 'L1_xattn_be3', 'L1_xattn_Wf1', 'L1_xattn_bf1',
        'L1_xattn_Wf2', 'L1_xattn_bf2', 'L1_ffn_router', 'L1_ffn_experts_gate', 'L1_ffn_experts_up',
        'L1_ffn_experts_down', 'L1_ffn_shared_gate', 'L1_ffn_shared_up', 'L1_ffn_shared_down']


def kernel(**inputs):
    import numpy as _np
    import concourse.bacc as _bacc
    from concourse import mybir as _mybir
    from concourse.bass_utils import run_bass_kernel_spmd as _run

    nc = _bacc.Bacc("TRN2", target_bir_lowering=False, num_devices=1)
    arrays, io = {}, {}
    for name in _INS:
        a = _np.ascontiguousarray(inputs[name])
        arrays[f"in_{name}_dram"] = a
        io[name] = nc.dram_tensor(f"in_{name}_dram", a.shape, _mybir.dt.from_np(a.dtype), kind="ExternalInput").ap()
    out = nc.dram_tensor("out_0_dram", (1, N, D), F32, kind="ExternalOutput").ap()
    transformer(nc, io, out)
    r = _run(nc, [arrays], core_ids=[0])
    return r.results[0]["out_0_dram"]
```

```python
from contextlib import ExitStack

import concourse.bass as bass
from concourse import mybir

F32 = mybir.dt.float32
BF16 = mybir.dt.bfloat16
U8 = mybir.dt.uint8
U32 = mybir.dt.uint32
ALU = mybir.AluOpType
ACT = mybir.ActivationFunctionType
AX_X = mybir.AxisListType.X

P = 128
N = 1024
NT = N // P
D = 128
H = 16
E = D // H
BANK = 512
HALVES = N // BANK
Q_PARTS = (0, 0, 0, 1, 1, 2)
K_PARTS = (0, 1, 2, 0, 1, 0)
TERMS = len(Q_PARTS)
ROW_MAX = TERMS * E
ROW_MASK = ROW_MAX + 3
BIG = 2.0 ** 127
EPS = 1e-5
NX = 8
DX = 64
CX = NX * DX // P
DMA = 16
VCOLS = 16


def ceil_div(a, b):
    return -(-a // b)


class Attention:
    pass


def attention_plan(name, keys, causal, masked, ring, lead, b_banks, p_slots):
    a = Attention()
    a.name, a.keys, a.causal, a.masked = name, keys, causal, masked
    a.ring, a.lead, a.b_banks, a.p_slots = ring, lead, b_banks, p_slots
    a.key_tiles = ceil_div(keys, P)
    wide = 2 * BANK
    a.segments = ceil_div(keys, wide)
    a.segment = min(wide, 4 * ceil_div(keys, 4 * a.segments))
    cut = a.segments // 2 * a.segment
    a.pieces = [(0, keys)] if keys <= wide else [(0, cut), (cut, keys)]
    if causal:
        a.max_units = [(qt, 0, (qt + 1) * P) for qt in range(NT)]
    else:
        a.max_units = [(qt, k0, min(a.segment, keys - k0))
                       for lo, hi in a.pieces for qt in range(NT) for k0 in range(lo, hi, a.segment)]
    a.units = []
    for kt in range(a.key_tiles):
        for half in range(HALVES):
            low = kt * P - half * BANK if causal else 0
            if low < BANK:
                a.units.append((kt, half, 0 if kt < 2 else max(0, low)))
    nb = len(a.units)
    a.piece_read = [sum(1 for kt, _, _ in a.units if kt * P < hi) for _, hi in a.pieces]
    a.batches = [list(range(u, u + 4 if u + 8 <= nb else nb)) for u in range(0, nb - 3, 4)]
    a.batch_of = {u: b for b, units in enumerate(a.batches) for u in units}
    lag = 3
    a.batch_at = [b[-1] + lag for b in a.batches]
    a.batch_at[0] = a.batch_at[1]
    a.tail = [b for b, at in enumerate(a.batch_at) if at >= nb]
    a.evacuate_at = max(a.batch_at[b] - nb for b in a.tail) + 1
    assert (ring * nb) % b_banks == 0 and (ring * nb) % p_slots == 0
    last = (nb * 92) // 100 if lead == 1 else nb
    total = sum(n for _, _, n in a.max_units)
    a.max_at, seen = [], 0
    for _, _, n in a.max_units:
        a.max_at.append(last * seen // total)
        seen += n
    a.turn_in_ring = lead == 1
    a.turn_at = last + max(1, nb // 34) if a.turn_in_ring else 3
    a.turn_unit = a.max_at.index(next(at for at in a.max_at if at >= a.turn_at)) if not a.turn_in_ring else None
    a.ring_uses = len(a.max_units) + a.turn_in_ring
    k_mode = "masked" if masked else "aside" if keys > wide else "plain"
    k_jobs = [("k", k_mode, c, min(BANK, keys - c)) for c in range(0, keys, BANK)]
    q_jobs = [("q", "plain", c * BANK, BANK) for c in range(HALVES)]
    a.jobs = k_jobs + q_jobs
    a.n_k_jobs = len(k_jobs)
    a.v_banks = [(t, min(4, a.key_tiles - t)) for t in range(0, a.key_tiles, 4)]
    return a


def transformer(nc, io, out):
    cross = {"ring": 2, "lead": 1, "b_banks": 3, "p_slots": 12}
    cross0 = attention_plan("cross0", 6404, causal=False, masked=True, **cross)
    self0 = attention_plan("self0", N, causal=False, masked=False, ring=4, lead=2, b_banks=2, p_slots=16)
    self1 = attention_plan("self1", N, causal=True, masked=False, ring=4, lead=2, b_banks=2, p_slots=12)
    cross1 = attention_plan("cross1", 6404, causal=False, masked=False, **cross)
    attentions = [cross0, self0, self1, cross1]
    S = cross0.keys
    KT = cross0.key_tiles
    FULL = S // P
    REST = S - FULL * P

    with ExitStack() as ctx:
        def sb(name, shape, dt=F32):
            return ctx.enter_context(nc.sbuf_tensor(name, shape, dt))

        def dram(name, shape, dt):
            return nc.dram_tensor(name, shape, dt, kind="Internal").ap()

        sems = {}

        def sem(name):
            if name not in sems:
                sems[name] = ctx.enter_context(nc.semaphore(name))
            return sems[name]

        ps = ctx.enter_context(nc.psum_tensor("ps", [P, 8, BANK], F32))
        A_BANK, B_BANK, TURN_BANK, ACC_BANK = 0, 4, 6, 7
        CTX_BANK, CTX_RING, CTX_AHEAD = 4, 4, 2

        x = sb("x", [P, NT, D])
        z = sb("z", [P, NT, D])
        xn = sb("xn", [P, NT, D])
        xT = sb("xT", [P, N])
        attT = sb("attT", [P, N])
        by_key = sb("by_key", [P, KT, D])
        ctxT = sb("ctxT", [P, S])
        k_stages = sb("k_stages", [P, 2 * S], BF16)
        qa_stage = sb("qa_stage", [P, 4, N], BF16)
        qb_stage = sb("qb_stage", [P, 4, N], BF16)
        v_stage = sb("v_stage", [P, 2, KT, VCOLS])

        def k_stage(a, slot):
            return k_stages[:, slot * a.keys:(slot + 1) * a.keys]

        probs = sb("probs", [P, 16, BANK])
        acc_out = sb("acc_out", [P, BANK])
        scratch = sb("scratch", [P, 8 * BANK])
        o_parts = scratch[:, 0:4 * BANK].rearrange("p (g q) -> p g q", g=4)
        den_parts = scratch[:, 4 * BANK:8 * BANK].rearrange("p (g q) -> p g q", g=4)
        maxima = sb("maxima", [P, NT, cross0.segments])
        neg_max = sb("neg_max", [P, NT])
        max_rest = sb("max_rest", [P, NT])
        max_parts = sb("max_parts", [P, 3, NT], BF16)
        max_rows = sb("max_rows", [3 * NT, P], BF16)
        SPLITS = 4
        probs_b = probs[:].rearrange("p a b -> p (a b)")
        keep = probs_b[:, 0:S // 2].bitcast(BF16)
        mask_in = probs_b[:, S // 2:S // 2 + S // 4].bitcast(U8)
        drop_row = k_stages[0:1, 0:S]
        part_words = SPLITS * 3 * BANK // 2
        for a in attentions:
            if a.masked:
                a.whole, a.rest = scratch[:, 0:SPLITS * BANK], scratch[:, SPLITS * BANK:2 * SPLITS * BANK]
                a.parts = probs_b[:, 16 * BANK - part_words:16 * BANK]
            else:
                a.whole, a.rest = probs_b[:, 0:SPLITS * BANK], probs_b[:, SPLITS * BANK:2 * SPLITS * BANK]
                a.parts = probs_b[:, 2 * SPLITS * BANK:2 * SPLITS * BANK + part_words]
            a.whole = a.whole.rearrange("p (b n) -> p b n", b=SPLITS)
            a.rest = a.rest.rearrange("p (b n) -> p b n", b=SPLITS)
            a.parts = a.parts.bitcast(BF16).rearrange("p (b t n) -> p b t n", b=SPLITS, t=3)
        assert S // 2 + S // 4 + part_words <= 16 * BANK
        hidden = probs_b[:, 0:5 * N].rearrange("p (c n) -> p c n", c=5)
        gated = probs_b[:, 5 * N:5 * N + 2 * 2 * BANK].rearrange("p (s b n) -> p s b n", s=2, b=2)
        stats = sb("stats", [P, NT, 6])
        mean_var = sb("mean_var", [P, NT, 2])
        var_eps = sb("var_eps", [P, NT])
        std = sb("std", [P, NT])
        rstd = sb("rstd", [P, NT])
        logits = sb("logits", [P, NT, NX])
        shifted = sb("shifted", [P, NT, NX])
        row_sum = sb("row_sum", [P, NT])
        top = sb("top", [P, NT, 8])
        top_at = sb("top_at", [P, NT, 8], U32)
        top_atf = sb("top_atf", [P, NT, 2])
        chosen = sb("chosen", [P, 2, NT, NX])
        coef = sb("coef", [P, NT, NX])
        top_w = sb("top_w", [P, 2, NT])
        coef_parts = sb("coef_parts", [P, NT, 3, NX], BF16)
        coefT = scratch[0:3 * NX, 0:N // 2].bitcast(BF16)
        ident = sb("ident", [P, P])
        ident_b = sb("ident_b", [P, P], BF16)
        causal_a = sb("causal_a", [P, P], BF16)
        causal_b = sb("causal_b", [P, 2 * P], BF16)
        expert_no = sb("expert_no", [P, NX])
        spread = sb("spread", [3 * NX, CX, P], BF16)
        ones_row = sb("ones_row", [1, N], BF16)
        two_ones = 1 + 2.0 ** -9 - 2.0 ** -16
        W = {}
        loads = []

        def weight(name, shape, source):
            W[name] = sb("w_" + name, shape)
            loads.append((W[name][:], source))

        def row_weight(name, source):
            weight(name, [P, D], source.partition_broadcast(P))

        weight("q_cross0", [P, D], io["L0_xattn_Wq"])
        weight("kv_cross0", [P, 2 * D], io["L0_xattn_Wkv"])
        n_first = len(loads)
        weight("o_cross0", [P, D], io["L0_xattn_Wproj"])
        row_weight("o_bias", io["L0_xattn_bproj"])
        weight("q_self0", [P, D], io["L0_ffn_Wq"])
        weight("k_self0", [P, D], io["L0_ffn_Wk"])
        weight("v_self0", [P, D], io["L0_ffn_Wv"])
        weight("o_self0", [P, D], io["L0_ffn_Wo"])
        for n in ("g1", "b1", "g2", "b2"):
            row_weight("m_" + n, io["L0_ffn_" + n])
        weight("gate0", [P, NX], io["L0_ffn_Wg"])
        weight("up0", [P, NX, DX], io["L0_ffn_W1"].rearrange("e d h -> d e h"))
        weight("down0", [P, CX, D], io["L0_ffn_W2"].rearrange("(c a) h d -> (a h) c d", a=P // DX))
        for n, a in (("1", "self1"), ("2", "cross1")):
            for m in "qkv":
                weight(f"{m}_{a}", [P, H, E], io[f"L1_xattn_W{m}{n}"].rearrange("h d e -> d h e"))
            weight("v_bias_" + a, [P, 1], io["L1_xattn_bv" + n].rearrange("h (e o) -> (h e) o", o=1))
        for n in ("g1", "be1", "g2", "be2", "g3", "be3"):
            row_weight("d_" + n, io["L1_xattn_" + n])
        weight("f1", [P, 4 * D], io["L1_xattn_Wf1"])
        weight("f1_bias", [P, 4], io["L1_xattn_bf1"].rearrange("(c p) -> p c", p=P))
        weight("f2", [P, 4, D], io["L1_xattn_Wf2"].rearrange("(c p) d -> p c d", p=P))
        row_weight("f2_bias", io["L1_xattn_bf2"])
        weight("router", [P, NX], io["L1_ffn_router"])
        weight("xgate", [P, NX, DX], io["L1_ffn_experts_gate"].rearrange("e d h -> d e h"))
        weight("xup", [P, NX, DX], io["L1_ffn_experts_up"].rearrange("e d h -> d e h"))
        weight("xdown", [P, CX, D], io["L1_ffn_experts_down"].rearrange("(c a) h d -> (a h) c d", a=P // DX))
        weight("sgate", [P, D], io["L1_ffn_shared_gate"])
        weight("sup", [P, D], io["L1_ffn_shared_up"])
        weight("sdown", [P, D], io["L1_ffn_shared_down"])

        def flat(w):
            return w[:] if len(w.shape) == 2 else w[:].rearrange("p a b -> p (a b)")

        for a in attentions:
            before = attentions[:attentions.index(a)]
            a.jobs_before = sum(len(b.jobs) for b in before)
            a.banks_before = sum(len(b.v_banks) for b in before)
            a.k_dram = dram("k_" + a.name, [3, P, a.keys], BF16)
            a.q_dram = dram("q_" + a.name, [H, TERMS * E, N], BF16)
            a.o_dram = dram("o_" + a.name, [4, 2, P, BANK], F32)

        def size(a, kt):
            return min(P, a.keys - kt * P)


        block = ctx.enter_context(nc.Block())

        def head_phases(eng, a, phase, steady=None):
            steady = H - 1 - a.lead if steady is None else steady
            rounds = steady // a.ring
            for h in range(-a.lead, 1):
                phase(h, h, 0)
            with eng.Fori(0, rounds) as turn:
                for r in range(1, a.ring + 1):
                    phase(turn * a.ring + r, r, turn)
            for h in range(1 + rounds * a.ring, H):
                phase(h, h, 0)

        def staged(a, r, piece):
            return sem(f"{a.name}_staged{piece}_{r % a.ring}")

        def stored(a, i):
            return sum(TERMS if a.jobs[j][0] == "q" else 1 for j in range(i % SPLITS, i + 1, SPLITS))

        @block.sync
        def _(sp):
            x_dram = io["x"].rearrange("a (t p) d -> p (a t) d", p=P)
            ctx_dram = io["ctx_1024"].rearrange("a s d -> (a s) d")
            sp.dma_start(x[:], x_dram).then_inc(sem("x_in"), DMA)
            for dst, src in loads[:n_first]:
                sp.dma_start(dst, src).then_inc(sem("first_weights_in"), DMA)
            for t in range(0, FULL, 4):
                n = min(4, FULL - t)
                sp.dma_start(by_key[:, t:t + n, :],
                             ctx_dram[t * P:(t + n) * P, :].rearrange("(t p) d -> p t d", p=P)
                             ).then_inc(sem(f"ctx_in{t // 4}"), DMA)
            sp.dma_start(by_key[0:REST, FULL, :], ctx_dram[FULL * P:S, :]).then_inc(sem("ctx_rest_in"), DMA)

            def load_mask_row():
                sp.wait_ge(sem("stages_cleared"), 1)
                sp.wait_ge(sem("drop_row_ready"), cross0.n_k_jobs)
                for b in range(2):
                    sp.dma_start(k_stages[ROW_MASK:ROW_MASK + 1, b * S:(b + 1) * S],
                                 drop_row).then_inc(sem("rows_in"), DMA)
                for q in (qa_stage, qb_stage):
                    for b in range(2):
                        sp.dma_start(q[ROW_MASK:ROW_MASK + 1, b, :], ones_row[:]).then_inc(sem("rows_in"), DMA)

            def clear_mask_row():
                for q in (qa_stage, qb_stage):
                    for b in range(2):
                        sp.dma_start(q[ROW_MASK:ROW_MASK + 1, b, :], qa_stage[P - 1:P, b, :]).then_inc(sem("rows_in"), DMA)
                sp.wait_ge(sem("rows_in"), 10 * DMA)

            def store_parts(a, first, last):
                for i in range(first, last):
                    kind, _, c0, n = a.jobs[i]
                    b = i % SPLITS
                    src, done = a.parts[:, b], sem(a.name + f"_stored{b}")
                    sp.wait_ge(sem("split_part3"), a.jobs_before + i + 1)
                    if kind == "k":
                        sp.dma_start(a.k_dram[:, :, c0:c0 + n].rearrange("a p c -> p a c"),
                                     src[:, :, 0:n]).then_inc(done, DMA)
                    else:
                        for term, part in enumerate(Q_PARTS):
                            sp.dma_start(a.q_dram[:, term * E:(term + 1) * E, c0:c0 + n],
                                         src[:, part, 0:n]).then_inc(done, DMA)

            def all_stored(a):
                for i in range(len(a.jobs) - SPLITS, len(a.jobs)):
                    sp.wait_ge(sem(a.name + f"_stored{i % SPLITS}"), DMA * stored(a, i))

            def attention(a):
                nb = len(a.units)
                last_piece = len(a.pieces) - 1

                def stage(h, r, piece):
                    lo, hi = a.pieces[piece]
                    slot, done = r % a.ring, staged(a, r, piece)
                    dst = k_stage(a, slot)
                    for row, parts_ in ((0, 3), (3 * E, 2), (5 * E, 1)):
                        sp.dma_start(dst[row:row + parts_ * E, lo:hi],
                                     a.k_dram[0:parts_, bass.ds(h * E, E), lo:hi]).then_inc(done, DMA)
                    if piece == 0:
                        sp.dma_start(qa_stage[0:ROW_MAX, slot, :], a.q_dram[h]).then_inc(done, DMA)
                    if piece == last_piece:
                        sp.dma_start(qb_stage[0:ROW_MAX, slot, :], a.q_dram[h]).then_inc(done, DMA)

                def put_maxima(h, r):
                    sp.wait_ge(sem(a.name + "_max_rows"), h + 1)
                    sp.dma_start(qb_stage[ROW_MAX:ROW_MASK, r % a.ring, :].rearrange("a (t q) -> a t q", t=NT),
                                 max_rows[:]).then_inc(sem(a.name + "_max_in"), DMA)

                def store_out(h):
                    sp.wait_ge(sem(a.name + "_acc_copied"), h + 1)
                    for g in range(4):
                        sp.dma_start(a.o_dram[g, :, bass.ds(h * E, E), :],
                                     acc_out[32 * g:32 * g + VCOLS, :]).then_inc(sem(a.name + "_acc_free"), DMA)

                def phase(h, r, turn):
                    if 1 <= r and r - 1 + a.ring < H:
                        sp.wait_ge(sem(a.name + "_scores"), h * nb)
                        stage(h - 1 + a.ring, r - 1 + a.ring, last_piece)
                    if a.turn_in_ring:
                        if 1 <= r:
                            store_out(h - 1)
                    elif 0 <= r + a.lead - 1 < H:
                        put_maxima(h + a.lead - 1, r + a.lead - 1)
                    if not a.turn_in_ring and 1 <= r:
                        store_out(h - 1)
                    for piece in range(last_piece):
                        if 0 <= r and r + a.ring < H:
                            sp.wait_ge(sem(a.name + "_scores"), h * nb + a.piece_read[piece])
                            stage(h + a.ring, r + a.ring, piece)
                    if a.turn_in_ring and r + a.lead < H:
                        put_maxima(h + a.lead, r + a.lead)

                for h in range(a.ring):
                    for piece in range(len(a.pieces)):
                        stage(h, h, piece)
                head_phases(sp, a, phase, steady=H - 1 - a.ring)

                def load_out(first, last):
                    sp.wait_ge(sem(a.name + "_acc_free"), (last + 1) * 4 * DMA)
                    rows = slice(first * E, last * E)
                    for kind, dst in enumerate((o_parts, den_parts)):
                        sp.dma_start(dst[rows], a.o_dram[:, kind, rows].rearrange("g p q -> p g q")
                                     ).then_inc(sem(a.name + "_out_in"), DMA)

                load_out(0, H - 1)
                store_out(H - 1)
                load_out(H - 1, H)

            for a in attentions:
                store_parts(a, 0, a.n_k_jobs)
                if a is cross0:
                    load_mask_row()
                store_parts(a, a.n_k_jobs, len(a.jobs))
                all_stored(a)
                if a is cross0:
                    sp.wait_ge(sem("rows_in"), 6 * DMA)
                attention(a)
                if a is cross0:
                    clear_mask_row()
            sp.wait_ge(sem("result_ready"), 1)
            sp.dma_start(out.rearrange("a (t p) d -> p (a t) d", p=P), xn[:]).then_inc(sem("result_out"), DMA)
            sp.wait_ge(sem("result_out"), DMA)

        @block.gpsimd
        def _(pool):
            chain = [0]

            def link(ins):
                chain[0] += 1
                ins.then_inc(sem("pool_chain"), 1)
                pool.wait_ge(sem("pool_chain"), chain[0])

            mask_bytes = io["mask_BxS2_bk0"].rearrange("a s -> (a s)").partition_broadcast(P)
            pool.dma_start(mask_in[:, 0:S], mask_bytes).then_inc(sem("mask_in"), DMA)
            link(nc.gpsimd.memset(ident[:], 0.0))
            nc.gpsimd.affine_select(out=ident[:], in_=ident[:], compare_op=ALU.not_equal, fill=1.0, base=0,
                                    pattern=[[-1, P]], channel_multiplier=1).then_inc(sem("ident_ready"), 1)
            pool.wait_ge(sem("ident_ready"), 1)
            nc.gpsimd.tensor_copy(ident_b[:], ident[:]).then_inc(sem("ident_ready"), 1)
            link(nc.gpsimd.memset(causal_a[:], 0.0))
            nc.gpsimd.affine_select(out=causal_a[:], in_=causal_a[:], compare_op=ALU.is_ge, fill=-BIG, base=0,
                                    pattern=[[-1, P]], channel_multiplier=1).then_inc(sem("masks_ready"), 1)
            link(nc.gpsimd.memset(causal_b[:], 0.0))
            nc.gpsimd.affine_select(out=causal_b[:], in_=causal_b[:], compare_op=ALU.is_ge, fill=-BIG, base=-P,
                                    pattern=[[1, 2 * P]], channel_multiplier=-1).then_inc(sem("masks_ready"), 1)
            for n in range(NX):
                nc.gpsimd.memset(expert_no[:, n:n + 1], float(n))
            hid = NX * DX
            bands = v_stage[:].rearrange("p s t c -> p (s t c)")[0:3 * NX, 0:3 * hid]
            link(nc.gpsimd.memset(bands, 1.0))
            link(nc.gpsimd.affine_select(out=bands, in_=bands, compare_op=ALU.is_ge, fill=0.0, base=0,
                                         pattern=[[1, 3 * hid]], channel_multiplier=-DX))
            link(nc.gpsimd.affine_select(out=bands, in_=bands, compare_op=ALU.is_ge, fill=0.0, base=DX - 1,
                                         pattern=[[-1, 3 * hid]], channel_multiplier=DX))
            link(nc.gpsimd.tensor_tensor(bands[:, 0:hid], bands[:, 0:hid], bands[:, hid:2 * hid], ALU.add))
            nc.gpsimd.tensor_tensor(spread[:].rearrange("p c m -> p (c m)"), bands[:, 0:hid],
                                    bands[:, 2 * hid:3 * hid], ALU.add).then_inc(sem("expert_consts"), 1)

            nc.gpsimd.memset(ones_row[:], 1.0)
            for q in (qa_stage, qb_stage):
                last = nc.gpsimd.memset(q[:].rearrange("p s n -> p (s n)").bitcast(F32), 0.0)
            last.then_inc(sem("stages_cleared"), 1)
            pool.wait_ge(sem("expert_consts"), 1)
            nc.gpsimd.memset(v_stage[:], 1.0).then_inc(sem("v_cleared"), 1)

            def split(a):
                for i, (kind, mode, c0, n) in enumerate(a.jobs):
                    b = i % SPLITS
                    if mode == "aside":
                        pool.wait_ge(sem("split_part1"), a.jobs_before + i + 1)
                        if i >= SPLITS:
                            pool.wait_ge(sem("split_part2"), a.jobs_before + i - SPLITS + 1)
                            pool.wait_ge(sem("split_part3"), a.jobs_before + i - SPLITS + 1)
                        nc.gpsimd.tensor_tensor(a.rest[:, b, 0:n], a.whole[:, b, 0:n], a.parts[:, b, 0, 0:n],
                                                ALU.subtract).then_inc(sem("split_rest"), 1)
                    pool.wait_ge(sem("split_part2"), a.jobs_before + i + 1)
                    nc.gpsimd.tensor_tensor(a.parts[:, b, 2, 0:n], a.rest[:, b, 0:n], a.parts[:, b, 1, 0:n],
                                            ALU.subtract).then_inc(sem("split_part3"), 1)

            def stage_values(a):
                nav = len(a.batches)

                def stage(h, par):
                    src = by_key[:, :, bass.ds(h * E, E)]
                    full = a.keys // P
                    nc.gpsimd.tensor_copy(v_stage[:, par, 0:full, 0:E],
                                          src[:, 0:full, :]).then_inc(sem(a.name + "_v_staged"), 1)
                    left = a.keys - full * P
                    if left:
                        nc.gpsimd.tensor_copy(v_stage[0:left, par, full, 0:E],
                                              src[0:left, full, :]).then_inc(sem(a.name + "_v_staged"), 1)

                pool.wait_ge(sem("values_ready"), a.banks_before + len(a.v_banks))
                stage(0, 0)
                stage(1, 1)
                if a is cross0:
                    for dst, src in loads[n_first:]:
                        pool.dma_start(dst, src, allow_slow_non_contiguous=True).then_inc(sem("weights_in"), DMA)
                with pool.Fori(0, (H - 2) // 2) as pair:
                    for par in range(2):
                        h = pair * 2 + 2 + par
                        pool.wait_ge(sem(a.name + "_batches"), (h - 1) * nav)
                        stage(h, par)

            pool.wait_ge(sem("v_cleared"), 1)
            for a in attentions:
                split(a)
                stage_values(a)

        @block.scalar
        def _(act):
            chain = [0]
            count = {"ln": 0, "turn": 0}

            def link(ins):
                chain[0] += 1
                ins.then_inc(sem("act_chain"), 1)
                act.wait_ge(sem("act_chain"), chain[0])

            def layer_norm():
                count["ln"] += 1
                act.wait_ge(sem("ln_variance"), count["ln"])
                nc.scalar.activation(std[:], var_eps[:], ACT.Sqrt).then_inc(sem("ln_std"), 1)

            def turned():
                count["turn"] += 1
                act.wait_ge(sem("turn_psum0"), count["turn"])
                nc.scalar.activation(xT[:, 0:BANK], ps[:, 6, :], ACT.Copy).then_inc(sem("turn_out"), 1)

            def evacuate_ctx(i):
                t, n = cross0.v_banks[i]
                act.wait_ge(sem("ctx_turned"), i + 1)
                w = min(S, (t + n) * P) - t * P
                nc.scalar.activation(ctxT[:, t * P:t * P + w], ps[:, CTX_BANK + i % CTX_RING, 0:w],
                                     ACT.Copy).then_inc(sem("ctxT_ready"), 1)

            def split(a, first, last):
                for i in range(first, last + 1):
                    if a is cross0:
                        for c in (range(CTX_AHEAD + 1) if i == 0 else [i + CTX_AHEAD]):
                            if c < len(a.v_banks):
                                evacuate_ctx(c)
                    if i < last:
                        kind, mode, c0, n = a.jobs[i]
                        b = i % SPLITS
                        src = ps[:, i % 3, 0:n] if mode == "plain" else a.whole[:, b, 0:n]
                        if mode == "masked":
                            act.wait_ge(sem(a.name + "_whole"), i + 1)
                        else:
                            act.wait_ge(sem("split_psum"), a.jobs_before + i + 1)
                        if i >= SPLITS:
                            act.wait_ge(sem(a.name + f"_stored{b}"), DMA * stored(a, i - SPLITS))
                        if mode == "aside":
                            if i >= SPLITS:
                                act.wait_ge(sem("split_rest"), a.jobs_before + i - SPLITS + 1)
                            nc.scalar.activation(src, ps[:, i % 3, 0:n], ACT.Copy).then_inc(sem(a.name + "_whole"), 1)
                            act.wait_ge(sem(a.name + "_whole"), i + 1)
                        nc.scalar.activation(a.parts[:, b, 0, 0:n], src, ACT.Copy).then_inc(sem("split_part1"), 1)
                    if i - 1 >= first:
                        _, _, _, n = a.jobs[i - 1]
                        b = (i - 1) % SPLITS
                        act.wait_ge(sem("split_rest"), a.jobs_before + i)
                        nc.scalar.activation(a.parts[:, b, 1, 0:n], a.rest[:, b, 0:n],
                                             ACT.Copy).then_inc(sem("split_part2"), 1)

            def values(a):
                for i, (t, n) in enumerate(a.v_banks):
                    act.wait_ge(sem("values_psum"), a.banks_before + i + 1)
                    src = ps[:, B_BANK + i % 2, 0:n * D].rearrange("p (t d) -> p t d", t=n)
                    full = n if (t + n) * P <= a.keys else n - 1
                    if full:
                        last = nc.scalar.activation(by_key[:, t:t + full, :], src[:, 0:full, :], ACT.Copy)
                    if full < n:
                        m = size(a, t + full)
                        last = nc.scalar.activation(by_key[0:m, t + full, :], src[0:m, full, :], ACT.Copy)
                    last.then_inc(sem("values_ready"), 1)

            def attention(a):
                nb, nav, done = len(a.units), len(a.batches), sem(a.name + "_probs")

                def evacuate(h):
                    act.wait_ge(sem(a.name + "_batches"), (h + 1) * nav)
                    act.wait_ge(sem(a.name + "_acc_free"), (h + 1) * 4 * DMA)
                    nc.scalar.activation(acc_out[:], ps[:, ACC_BANK, :],
                                         ACT.Copy).then_inc(sem(a.name + "_acc_copied"), 1)

                def phase(h, r, turn):
                    if r < 0:
                        return
                    for u, (kt, half, low) in enumerate(a.units):
                        m = size(a, kt)
                        slot = (r * nb + u) % a.p_slots
                        bank = B_BANK + (r * nb + u) % a.b_banks
                        act.wait_ge(sem(a.name + "_scores"), h * nb + u + 1)
                        if u >= a.p_slots:
                            if (u - a.p_slots) % 4 == 0:
                                act.wait_ge(sem(a.name + "_batches"), h * nav + a.batch_of[u - a.p_slots] + 1)
                        elif r >= 1:
                            old = nb + u - a.p_slots
                            if old % 4 == 0 or u == 0:
                                act.wait_ge(sem(a.name + "_batches"), (h - 1) * nav + a.batch_of[old] + 1)
                        nc.scalar.activation(probs[0:m, slot, low:BANK], ps[0:m, bank, low:BANK], ACT.Exp,
                                             scale=float(E) ** -0.5).then_inc(done, 1)
                        if r >= 1 and u == a.evacuate_at:
                            evacuate(h - 1)

                values(a)
                head_phases(act, a, phase)
                evacuate(H - 1)

            layer_norm()
            turned()
            for a in attentions:
                if a is cross1:
                    split(a, 0, a.n_k_jobs)
                if a is self0 or a is cross1:
                    layer_norm()
                if a is self0 or a is self1:
                    layer_norm()
                if a is not cross0:
                    turned()
                split(a, a.n_k_jobs if a is cross1 else 0, len(a.jobs))
                attention(a)
                if a is self0:
                    layer_norm()
                    turned()
                    act.wait_ge(sem("moe0_gap"), 1)
                    nc.scalar.activation(top_w[:, 1, :], top_w[:, 0, :], ACT.Exp).then_inc(sem("moe0_exp"), 1)
                    for u in range(CX * HALVES):
                        act.wait_ge(sem("moe0_up"), u + 1)
                        if u >= 2:
                            act.wait_ge(sem("moe0_hidden"), u - 1)
                        nc.scalar.activation(gated[:, u % 2, 0, :], ps[:, 3 * (u % 2), :],
                                             ACT.Relu).then_inc(sem("moe0_relu"), 1)
                if a is cross1:
                    layer_norm()
                    turned()
                    for u in range(4 * HALVES):
                        c, half = u // HALVES, u % HALVES
                        act.wait_ge(sem("ffn_up"), u + 1)
                        nc.scalar.activation(hidden[:, c, half * BANK:(half + 1) * BANK], ps[:, u % 4, :], ACT.Relu,
                                             bias=W["f1_bias"][:, c:c + 1]).then_inc(sem("ffn_hidden"), 1)
                    layer_norm()
                    layer_norm()
                    turned()
                    act.wait_ge(sem("moe1_shift"), 1)
                    nc.scalar.activation(logits[:], shifted[:], ACT.Exp).then_inc(sem("moe1_exp"), 1)
                    for u in range((CX + 1) * HALVES):
                        act.wait_ge(sem("moe1_up"), u + 1)
                        if u >= 2:
                            act.wait_ge(sem("moe1_hidden"), u - 1)
                        nc.scalar.activation(gated[:, u % 2, 0, :], ps[:, 3 * (u % 2), :],
                                             ACT.Silu).then_inc(sem("moe1_silu"), 1)

        @block.vector
        def _(dve):
            chain = [0]
            count = {"ln": 0, "turn": 0}

            def link(ins):
                chain[0] += 1
                ins.then_inc(sem("dve_chain"), 1)
                dve.wait_ge(sem("dve_chain"), chain[0])

            def tt(out_, a, b, op):
                return nc.vector.tensor_tensor(out_, a, b, op)

            def layer_norm(dst, src, gain=None, bias=None):
                count["ln"] += 1
                for t in range(NT):
                    last = nc.vector.bn_stats(stats[:, t, :], src[:, t, :])
                link(last)
                for t in range(NT):
                    last = nc.vector.bn_aggr(mean_var[:, t, :], stats[:, t, :])
                link(last)
                nc.vector.tensor_scalar(var_eps[:], mean_var[:, :, 1], EPS, None,
                                        ALU.add).then_inc(sem("ln_variance"), 1)
                dve.wait_ge(sem("ln_std"), count["ln"])
                link(nc.vector.reciprocal(rstd[:], std[:]))
                for t in range(NT):
                    last = nc.vector.tensor_scalar(dst[:, t, :], src[:, t, :], mean_var[:, t, 0:1], rstd[:, t:t + 1],
                                                   ALU.subtract, ALU.mult)
                if gain is not None:
                    link(last)
                    link(tt(dst[:], dst[:], W[gain][:].unsqueeze(1).to_broadcast([P, NT, D]), ALU.mult))
                    last = tt(dst[:], dst[:], W[bias][:].unsqueeze(1).to_broadcast([P, NT, D]), ALU.add)
                last.then_inc(sem("ln_out"), 1)
                dve.wait_ge(sem("ln_out"), count["ln"])

            def turned():
                count["turn"] += 1
                dve.wait_ge(sem("turn_psum1"), count["turn"])
                nc.vector.tensor_copy(xT[:, BANK:N], ps[:, 7, :]).then_inc(sem("turn_out"), 1)

            def split(a):

                def take_rest(i):
                    _, mode, _, n = a.jobs[i]
                    b = i % SPLITS
                    if mode == "aside":
                        return
                    src = ps[:, i % 3, 0:n] if mode == "plain" else a.whole[:, b, 0:n]
                    dve.wait_ge(sem("split_part1"), a.jobs_before + i + 1)
                    if i >= SPLITS:
                        dve.wait_ge(sem("split_part3"), a.jobs_before + i - SPLITS + 1)
                    tt(a.rest[:, b, 0:n], src, a.parts[:, b, 0, 0:n], ALU.subtract).then_inc(sem("split_rest"), 1)

                if a.masked:
                    make_keep(0)
                for i, (kind, mode, c0, n) in enumerate(a.jobs):
                    if mode == "masked":
                        if i + 1 < a.n_k_jobs:
                            make_keep(i + 1)
                        dve.wait_ge(sem("keep_ready"), i + 1)
                        nc.vector.tensor_scalar(drop_row[:, c0:c0 + n], keep[0:1, c0:c0 + n], BIG, -BIG,
                                                ALU.mult, ALU.add).then_inc(sem("drop_row_ready"), 1)
                        dve.wait_ge(sem("split_psum"), a.jobs_before + i + 1)
                        if i >= SPLITS:
                            dve.wait_ge(sem("split_rest"), a.jobs_before + i - SPLITS + 1)
                        tt(a.whole[:, i % SPLITS, 0:n], ps[:, i % 3, 0:n], keep[:, c0:c0 + n],
                           ALU.mult).then_inc(sem(a.name + "_whole"), 1)
                    if i >= 1:
                        take_rest(i - 1)
                take_rest(len(a.jobs) - 1)

            def make_keep(i):
                _, _, c0, n = cross0.jobs[i]
                nc.vector.tensor_scalar(keep[:, c0:c0 + n], mask_in[:, c0:c0 + n], -1.0, 1.0,
                                        ALU.mult, ALU.add).then_inc(sem("keep_ready"), 1)

            def attention(a):
                uses, step = a.ring_uses, sem(a.name + "_max_step")
                STEPS = 5

                def take_turned(h, r):
                    if a.turn_in_ring:
                        bank = A_BANK + 2 * ((r * uses + uses - 1) % 2)
                        dve.wait_ge(sem(a.name + "_max_scores"), (h + 1) * uses)
                    else:
                        bank = TURN_BANK
                        dve.wait_ge(sem(a.name + "_turned"), h + 1)
                    if r >= 1:
                        dve.wait_ge(sem(a.name + "_max_in"), h * DMA)
                    nc.vector.tensor_copy(max_rows[:], ps[0:3 * NT, bank, 0:P // 2].bitcast(BF16)
                                          ).then_inc(sem(a.name + "_max_rows"), 1)

                def phase(h_now, r_now, turn):
                    h, r = h_now + a.lead, r_now + a.lead
                    if r == H and not a.turn_in_ring:
                        take_turned(h - 1, r - 1)
                    if r >= H:
                        return
                    for u, (qt, k0, n) in enumerate(a.max_units):
                        if u == a.turn_unit and r >= 1:
                            take_turned(h - 1, r - 1)
                        b = (r * uses + u) % 2
                        seg = k0 // a.segment
                        dve.wait_ge(sem(a.name + "_max_scores"), h * uses + u + 1)
                        nc.vector.tensor_reduce(maxima[:, qt, seg:seg + 1],
                                                ps[:, A_BANK + 2 * b:A_BANK + 2 * b + 2, :].rearrange(
                                                    "p a b -> p (a b)")[:, 0:n],
                                                AX_X, ALU.max).then_inc(sem(a.name + "_max_read"), 1)
                    dve.wait_ge(sem(a.name + "_max_read"), h * len(a.max_units) + len(a.max_units))

                    def linked(k, ins):
                        ins.then_inc(step, 1)
                        dve.wait_ge(step, h * STEPS + k)

                    linked(1, nc.vector.tensor_reduce(neg_max[:], maxima[:, :, 0:a.segments], AX_X, ALU.max,
                                                      negate=True))
                    linked(2, nc.vector.tensor_copy(max_parts[:, 0, :], neg_max[:]))
                    linked(3, tt(max_rest[:], neg_max[:], max_parts[:, 0, :], ALU.subtract))
                    linked(4, nc.vector.tensor_copy(max_parts[:, 1, :], max_rest[:]))
                    tt(max_parts[:, 2, :], max_rest[:], max_parts[:, 1, :], ALU.subtract).then_inc(step, 1)
                    if a.turn_in_ring:
                        take_turned(h, r)

                head_phases(dve, a, phase)
                dve.wait_ge(sem(a.name + "_out_in"), 4 * DMA)
                o, den = o_parts, den_parts
                for half in range(HALVES):
                    tt(o[:, half, :], o[:, half, :], o[:, 2 + half, :], ALU.add)
                    summed = tt(den[:, half, :], den[:, half, :], den[:, 2 + half, :], ALU.add)
                link(summed)
                for half in range(HALVES):
                    cols = attT[:, half * BANK:(half + 1) * BANK]
                    link(nc.vector.reciprocal(den[:, 2 + half, :], den[:, half, :]))
                    last = tt(cols, o[:, half, :], den[:, 2 + half, :], ALU.mult)
                    if "v_bias_" + a.name in W:
                        link(last)
                        last = nc.vector.tensor_scalar(cols, cols, W["v_bias_" + a.name][:], None, ALU.add)
                    last.then_inc(sem("attended"), 1)

            def add_result(name, dst, other, bias=None):
                for b in range(2):
                    dve.wait_ge(sem(name), b + 1)
                    ins = tt(dst[:, 4 * b:4 * b + 4, :], ps[:, 6 + b, :].rearrange("p (t d) -> p t d", t=4),
                             other[:, 4 * b:4 * b + 4, :], ALU.add)
                link(ins)
                if bias is not None:
                    link(tt(dst[:], dst[:], W[bias][:].unsqueeze(1).to_broadcast([P, NT, D]), ALU.add))

            def top_two(values):
                for t in range(NT):
                    last = nc.vector.max(top[:, t, :], values[:, t, :])
                link(last)
                for t in range(NT):
                    last = nc.vector.max_index(top_at[:, t, :], top[:, t, :], values[:, t, :])
                link(last)
                link(nc.vector.tensor_copy(top_atf[:], top_at[:, :, 0:2]))
                for k in range(2):
                    last = tt(chosen[:, k], expert_no[:].unsqueeze(1).to_broadcast([P, NT, NX]),
                              top_atf[:, :, k].unsqueeze(2).to_broadcast([P, NT, NX]), ALU.is_equal)
                link(last)

            def weigh(w0, w1):
                tt(chosen[:, 0], chosen[:, 0], w0.unsqueeze(2).to_broadcast([P, NT, NX]), ALU.mult)
                link(tt(chosen[:, 1], chosen[:, 1], w1.unsqueeze(2).to_broadcast([P, NT, NX]), ALU.mult))
                link(tt(coef[:], chosen[:, 0], chosen[:, 1], ALU.add))
                rest = chosen[:, 0]
                link(nc.vector.tensor_copy(coef_parts[:, :, 0, :], coef[:]))
                link(tt(rest, coef[:], coef_parts[:, :, 0, :], ALU.subtract))
                link(nc.vector.tensor_copy(coef_parts[:, :, 1, :], rest))
                tt(coef_parts[:, :, 2, :], rest, coef_parts[:, :, 1, :], ALU.subtract).then_inc(sem("coef_ready"), 1)

            def coef_turned(k):
                for b in range(2):
                    dve.wait_ge(sem("coef_psum"), 2 * k + b + 1)
                    nc.vector.tensor_copy(coefT[:, b * BANK:(b + 1) * BANK],
                                          ps[0:3 * NX, 6 + b, 0:BANK // 2].bitcast(BF16)
                                          ).then_inc(sem("coefT_ready"), 1)

            nc.vector.memset(ps[:, ACC_BANK, :], 0.0).then_inc(sem("acc_cleared"), 1)
            for i, a in reversed(list(enumerate(attentions))):
                nc.vector.memset(acc_out[:, i * P:(i + 1) * P], 0.0).then_inc(sem(a.name + "_acc_free"), 4 * DMA)
            nc.vector.memset(k_stages[:].bitcast(F32), two_ones).then_inc(sem("k_stages_cleared"), 1)
            dve.wait_ge(sem("x_in"), DMA)
            layer_norm(xn, x)
            turned()
            dve.wait_ge(sem("mask_in"), DMA)
            dve.wait_ge(sem("k_stages_cleared"), 1)
            split(cross0)
            attention(cross0)
            add_result("cross0_result", x, x, "o_bias")

            layer_norm(z, x)
            layer_norm(xn, z, "m_g1", "m_b1")
            turned()
            split(self0)
            attention(self0)
            add_result("self0_result", z, z)
            layer_norm(xn, z, "m_g2", "m_b2")
            turned()
            dve.wait_ge(sem("gate_logits"), 1)
            link(nc.vector.tensor_copy(logits[:].rearrange("p t e -> p (t e)"), ps[:, 5, 0:NT * NX]))
            top_two(logits)
            tt(top_w[:, 0, :], top[:, :, 1], top[:, :, 0], ALU.subtract).then_inc(sem("moe0_gap"), 1)
            dve.wait_ge(sem("moe0_exp"), 1)
            link(nc.vector.tensor_scalar(row_sum[:], top_w[:, 1, :], 1.0, None, ALU.add))
            link(nc.vector.reciprocal(top_w[:, 0, :], row_sum[:]))
            link(tt(top_w[:, 1, :], top_w[:, 1, :], top_w[:, 0, :], ALU.mult))
            weigh(top_w[:, 0, :], top_w[:, 1, :])
            coef_turned(0)
            for u in range(CX * HALVES):
                c, half = u // HALVES, u % HALVES
                dve.wait_ge(sem("moe0_relu"), u + 1)
                tt(hidden[:, c, half * BANK:(half + 1) * BANK], ps[:, 3 * (u % 2) + 1, :], gated[:, u % 2, 0, :],
                   ALU.mult).then_inc(sem("moe0_hidden"), 1)
            add_result("moe0_result", z, z)
            link(tt(x[:], x[:], z[:], ALU.add))

            layer_norm(z, x)
            turned()
            split(self1)
            attention(self1)
            add_result("self1_result", z, z)
            layer_norm(z, z, "d_g1", "d_be1")
            turned()
            split(cross1)
            attention(cross1)
            add_result("cross1_result", z, z)
            layer_norm(z, z, "d_g2", "d_be2")
            turned()
            add_result("ffn_result", z, z, "f2_bias")
            layer_norm(z, z, "d_g3", "d_be3")
            link(tt(x[:], x[:], z[:], ALU.add))

            layer_norm(z, x)
            turned()
            dve.wait_ge(sem("gate_logits"), 2)
            link(nc.vector.tensor_copy(logits[:].rearrange("p t e -> p (t e)"), ps[:, 5, 0:NT * NX]))
            link(nc.vector.tensor_reduce(row_sum[:], logits[:], AX_X, ALU.max))
            tt(shifted[:], logits[:], row_sum[:].unsqueeze(2).to_broadcast([P, NT, NX]),
               ALU.subtract).then_inc(sem("moe1_shift"), 1)
            dve.wait_ge(sem("moe1_exp"), 1)
            link(nc.vector.tensor_reduce(row_sum[:], logits[:], AX_X, ALU.add))
            link(nc.vector.reciprocal(top_w[:, 0, :], row_sum[:]))
            link(tt(logits[:], logits[:], top_w[:, 0, :].unsqueeze(2).to_broadcast([P, NT, NX]), ALU.mult))
            top_two(logits)
            weigh(top[:, :, 0], top[:, :, 1])
            coef_turned(1)
            for u in range((CX + 1) * HALVES):
                c, half = u // HALVES, u % HALVES
                dst = hidden[:, c, half * BANK:(half + 1) * BANK]
                dve.wait_ge(sem("moe1_silu"), u + 1)
                first = 3 * (u % 2)
                if c < CX:
                    link(tt(gated[:, u % 2, 1, :], ps[:, first + 1, :], gated[:, u % 2, 0, :], ALU.mult))
                    ins = tt(dst, ps[:, first + 2, :], gated[:, u % 2, 1, :], ALU.mult)
                else:
                    ins = tt(dst, ps[:, first + 1, :], gated[:, u % 2, 0, :], ALU.mult)
                ins.then_inc(sem("moe1_hidden"), 1)
            for b in range(2):
                dve.wait_ge(sem("moe1_result"), b + 1)
                ins = tt(xn[:, 4 * b:4 * b + 4, :], ps[:, 6 + b, :].rearrange("p (t d) -> p t d", t=4),
                         x[:, 4 * b:4 * b + 4, :], ALU.add)
            ins.then_inc(sem("result_ready"), 1)

        @block.tensor
        def _(pe):
            count = {"turn": 0}

            def mm(out_, lhsT, rhs, start=True, stop=True):
                return nc.tensor.matmul(out_, lhsT, rhs, start=start, stop=stop)

            def turn(src, ln):
                count["turn"] += 1
                pe.wait_ge(sem("ln_out"), ln)
                for b in range(2):
                    for t in range(4):
                        last = nc.tensor.transpose(ps[:, 6 + b, t * P:(t + 1) * P], src[:, 4 * b + t, :], ident[:])
                    last.then_inc(sem(f"turn_psum{b}"), 1)
                pe.wait_ge(sem("turn_out"), 2 * count["turn"])

            def project(a, w_q, w_k, kT, first, last, before=None):
                for i in range(first, last):
                    if before:
                        before(i)
                    kind, mode, c0, n = a.jobs[i]
                    if i >= 3:
                        if a.jobs[i - 3][1] == "plain":
                            pe.wait_ge(sem("split_rest"), a.jobs_before + i - 2)
                        else:
                            pe.wait_ge(sem(a.name + "_whole"), i - 2)
                    src, w = (xT, w_q) if kind == "q" else (kT, w_k)
                    mm(ps[:, i % 3, 0:n], w, src[:, c0:c0 + n]).then_inc(sem("split_psum"), 1)

            def attention(a, kT, w_v):
                nb, uses, nav = len(a.units), a.ring_uses, len(a.batches)
                n_max = len(a.max_units)
                last_unit = {}
                for u, (kt, half, low) in enumerate(a.units):
                    last_unit[(kt % 2, half)] = u

                def project_values(i):
                    t, n = a.v_banks[i]
                    if i >= 2:
                        pe.wait_ge(sem("values_ready"), a.banks_before + i - 1)
                    for j in range(n):
                        m = size(a, t + j)
                        last = mm(ps[0:m, B_BANK + i % 2, j * D:(j + 1) * D], kT[:, (t + j) * P:(t + j) * P + m], w_v)
                    last.then_inc(sem("values_psum"), 1)

                def ring_free(h, r, u):
                    if a.turn_in_ring and u < 2 and r >= 1:
                        if u == 1:
                            pe.wait_ge(sem(a.name + "_max_rows"), h)
                        else:
                            pe.wait_ge(sem(a.name + "_max_read"), h * n_max)
                    elif r >= 1 or u >= 2:
                        pe.wait_ge(sem(a.name + "_max_read"), h * n_max + u - 1)

                def pass_a(h, r, u, turn):
                    qt, k0, n = a.max_units[u]
                    b = (r * uses + u) % 2
                    for piece, (lo, _) in enumerate(a.pieces):
                        if k0 == lo and qt == 0:
                            dmas = 3 + (piece == 0) + (piece == len(a.pieces) - 1)
                            pe.wait_ge(staged(a, r, piece), (turn + r // a.ring + 1) * dmas * DMA)
                    ring_free(h, r, u)
                    q, k = qa_stage[:, r % a.ring, qt * P:(qt + 1) * P], k_stage(a, r % a.ring)
                    for c in range(0, n, BANK):
                        w = min(BANK, n - c)
                        diag = a.causal and c + w == n
                        bank = A_BANK + 2 * b + c // BANK
                        last = mm(ps[:, bank, 0:w], q, k[:, k0 + c:k0 + c + w], stop=not diag)
                        if diag:
                            last = mm(ps[:, bank, w - P:w], ident_b[:], causal_a[:], start=False)
                    last.then_inc(sem(a.name + "_max_scores"), 1)

                def turn_maxima(h, r):
                    pe.wait_ge(sem(a.name + "_max_step"), (h + 1) * 5)
                    if a.turn_in_ring:
                        bank, done = A_BANK + 2 * ((r * uses + uses - 1) % 2), "_max_scores"
                        pe.wait_ge(sem(a.name + "_max_read"), (h + 1) * n_max - 1)
                    else:
                        bank, done = TURN_BANK, "_turned"
                        if r >= 1:
                            pe.wait_ge(sem(a.name + "_max_rows"), h)
                    nc.tensor.transpose(ps[0:3 * NT, bank, 0:P // 2].bitcast(BF16),
                                        max_parts[:].rearrange("p a t -> p (a t)"),
                                        ident_b[:]).then_inc(sem(a.name + done), 1)

                def pass_b(h, r, u):
                    kt, half, low = a.units[u]
                    m = size(a, kt)
                    bank = B_BANK + (r * nb + u) % a.b_banks
                    if u == 0:
                        pe.wait_ge(sem(a.name + "_max_in"), (h + 1) * DMA)
                        if r == 0:
                            pe.wait_ge(sem("values_ready"), a.banks_before + len(a.v_banks))
                    if r >= 1 or u >= a.b_banks:
                        pe.wait_ge(sem(a.name + "_probs"), h * nb + u + 1 - a.b_banks)
                    diag = a.causal and kt // 4 == half
                    slot = r % a.ring
                    last = mm(ps[0:m, bank, low:BANK], k_stage(a, slot)[:, kt * P:kt * P + m],
                              qb_stage[:, slot, half * BANK + low:(half + 1) * BANK], stop=not diag)
                    if diag:
                        hi = (kt % 4 + 1) * P
                        last = mm(ps[:, bank, low:hi], ident_b[:], causal_b[:, 2 * P - (hi - low):2 * P],
                                  start=False)
                    last.then_inc(sem(a.name + "_scores"), 1)

                def values(h, r, b):
                    units = a.batches[b]
                    pe.wait_ge(sem(a.name + "_probs"), h * nb + units[-1] + 1)
                    if b == 0:
                        pe.wait_ge(sem(a.name + "_v_staged"), (h + 1) * (1 if a.keys % P == 0 else 2))
                        if r >= 1:
                            pe.wait_ge(sem(a.name + "_acc_copied"), h)
                    for u in units:
                        kt, half, low = a.units[u]
                        m = size(a, kt)
                        g = (kt % 2) * 2 + half
                        last = mm(ps[32 * g:32 * g + VCOLS, ACC_BANK, low:BANK], v_stage[0:m, r % 2, kt, :],
                                  probs[0:m, (r * nb + u) % a.p_slots, low:BANK],
                                  start=kt < 2, stop=u == last_unit[(kt % 2, half)])
                    last.then_inc(sem(a.name + "_batches"), 1)

                def phase(h, r, turn):
                    ahead, r_ahead = h + a.lead, r + a.lead
                    if r < 0:
                        for u in range(n_max):
                            if not a.turn_in_ring and u == a.turn_unit and r_ahead >= 1:
                                turn_maxima(ahead - 1, r_ahead - 1)
                            pass_a(ahead, r_ahead, u, turn)
                            if r_ahead == 0:
                                nv = len(a.v_banks)
                                for i in range(u * nv // n_max, (u + 1) * nv // n_max):
                                    project_values(i)
                        if a.turn_in_ring:
                            turn_maxima(ahead, r_ahead)
                        return
                    for u in range(nb):
                        pass_b(h, r, u)
                        if r >= 1:
                            for b in a.tail:
                                if a.batch_at[b] - nb == u:
                                    values(h - 1, r - 1, b)
                        for b in range(nav):
                            if a.batch_at[b] == u:
                                values(h, r, b)
                        turn_now = u == a.turn_at
                        if turn_now and not a.turn_in_ring and r_ahead <= H:
                            turn_maxima(ahead - 1, r_ahead - 1)
                        if r_ahead < H:
                            for v, at in enumerate(a.max_at):
                                if at == u:
                                    pass_a(ahead, r_ahead, v, turn)
                            if turn_now and a.turn_in_ring:
                                turn_maxima(ahead, r_ahead)

                head_phases(pe, a, phase)
                for b in a.tail:
                    values(H - 1, H - 1, b)

            def out_tiles(name, pairs, attended=None):
                for b in range(2):
                    if attended is not None:
                        pe.wait_ge(sem("attended"), 2 * attended + b + 1)
                    for t in range(4 * b, 4 * b + 4):
                        for i, (lhs, rhs) in enumerate(pairs):
                            last = mm(ps[:, 6 + b, (t % 4) * D:(t % 4 + 1) * D], lhs[:, t * P:(t + 1) * P], rhs,
                                      start=i == 0, stop=i == len(pairs) - 1)
                    last.then_inc(sem(name), 1)

            def turn_back(name, attended):
                for b in range(2):
                    pe.wait_ge(sem("attended"), 2 * attended + b + 1)
                    for t in range(4):
                        last = nc.tensor.transpose(ps[:, 6 + b, t * P:(t + 1) * P],
                                                   attT[:, (4 * b + t) * P:(4 * b + t + 1) * P], ident[:])
                    last.then_inc(sem(name), 1)

            def gate(w):
                for t in range(NT):
                    last = mm(ps[:, 5, t * NX:(t + 1) * NX], xT[:, t * P:(t + 1) * P], w)
                last.then_inc(sem("gate_logits"), 1)

            def turn_coef(k):
                pe.wait_ge(sem("coef_ready"), k + 1)
                for b in range(2):
                    for t in range(4):
                        last = nc.tensor.transpose(ps[0:3 * NX, 6 + b, t * P // 2:(t + 1) * P // 2].bitcast(BF16),
                                                   coef_parts[:, 4 * b + t].rearrange("p a e -> p (a e)"), ident_b[:])
                    last.then_inc(sem("coef_psum"), 1)
                pe.wait_ge(sem("coefT_ready"), 2 * (k + 1))

            pe.wait_ge(sem("ident_ready"), 2)
            pe.wait_ge(sem("acc_cleared"), 1)
            turn(xn, 1)
            pe.wait_ge(sem("first_weights_in"), DMA * n_first)

            def turn_context(i):
                t, n = cross0.v_banks[i]
                if i >= CTX_RING:
                    pe.wait_ge(sem("ctxT_ready"), i - CTX_RING + 1)
                for j in range(n):
                    m = size(cross0, t + j)
                    if (t + j) % 4 == 0 and m == P:
                        pe.wait_ge(sem(f"ctx_in{(t + j) // 4}"), DMA)
                    if m < P:
                        pe.wait_ge(sem("ctx_rest_in"), DMA)
                    last = nc.tensor.transpose(ps[:, CTX_BANK + i % CTX_RING, j * P:j * P + m], by_key[0:m, t + j, :],
                                               ident[0:m, 0:m])
                last.then_inc(sem("ctx_turned"), 1)

            def cross0_before(i):
                for b in (range(CTX_AHEAD + 1) if i == 0 else [i + CTX_AHEAD]):
                    if b < len(cross0.v_banks):
                        turn_context(b)
                pe.wait_ge(sem("ctxT_ready"), min(i, len(cross0.v_banks) - 1) + 1)

            kv = W["kv_cross0"]
            project(cross0, W["q_cross0"][:], kv[:, 0:D], ctxT, 0, len(cross0.jobs), before=cross0_before)
            pe.wait_ge(sem("rows_in"), 6 * DMA)
            attention(cross0, ctxT, kv[:, D:2 * D])
            pe.wait_ge(sem("weights_in"), DMA * (len(loads) - n_first))
            out_tiles("cross0_result", [(attT, W["o_cross0"][:])], attended=0)

            turn(xn, 3)
            project(self0, W["q_self0"][:], W["k_self0"][:], xT, 0, len(self0.jobs))
            pe.wait_ge(sem("rows_in"), 10 * DMA)
            attention(self0, xT, W["v_self0"][:])
            out_tiles("self0_result", [(attT, W["o_self0"][:])], attended=1)
            turn(xn, 4)
            gate(W["gate0"][:])
            pe.wait_ge(sem("expert_consts"), 1)
            turn_coef(0)
            for u in range(CX * HALVES):
                c, half = u // HALVES, u % HALVES
                if u >= 2:
                    pe.wait_ge(sem("moe0_hidden"), u - 1)
                cols = slice(half * BANK, (half + 1) * BANK)
                mm(ps[:, 3 * (u % 2) + 1, :], spread[:, c, :], coefT[:, cols])
                mm(ps[:, 3 * (u % 2), :], flat(W["up0"])[:, c * P:(c + 1) * P], xT[:, cols]).then_inc(sem("moe0_up"), 1)
            pe.wait_ge(sem("moe0_hidden"), CX * HALVES)
            out_tiles("moe0_result", [(hidden[:, c, :], W["down0"][:, c, :]) for c in range(CX)])

            turn(z, 5)
            pe.wait_ge(sem("masks_ready"), 2)
            project(self1, flat(W["q_self1"]), flat(W["k_self1"]), xT, 0, len(self1.jobs))
            attention(self1, xT, flat(W["v_self1"]))
            project(cross1, flat(W["q_cross1"]), flat(W["k_cross1"]), ctxT, 0, cross1.n_k_jobs)
            turn_back("self1_result", 2)
            turn(z, 6)
            project(cross1, flat(W["q_cross1"]), flat(W["k_cross1"]), ctxT, cross1.n_k_jobs, len(cross1.jobs))
            attention(cross1, ctxT, flat(W["v_cross1"]))
            turn_back("cross1_result", 3)
            turn(z, 7)
            for u in range(4 * HALVES):
                c, half = u // HALVES, u % HALVES
                if u >= 4:
                    pe.wait_ge(sem("ffn_hidden"), u - 3)
                mm(ps[:, u % 4, :], W["f1"][:, c * P:(c + 1) * P],
                   xT[:, half * BANK:(half + 1) * BANK]).then_inc(sem("ffn_up"), 1)
            pe.wait_ge(sem("ffn_hidden"), 4 * HALVES)
            out_tiles("ffn_result", [(hidden[:, c, :], W["f2"][:, c, :]) for c in range(4)])
            turn(z, 9)
            gate(W["router"][:])
            turn_coef(1)
            for u in range((CX + 1) * HALVES):
                c, half = u // HALVES, u % HALVES
                if u >= 2:
                    pe.wait_ge(sem("moe1_hidden"), u - 1)
                cols = slice(half * BANK, (half + 1) * BANK)
                first = 3 * (u % 2)
                if c < CX:
                    mm(ps[:, first + 2, :], spread[:, c, :], coefT[:, cols])
                    w_up, w_gate = (flat(W[n])[:, c * P:(c + 1) * P] for n in ("xup", "xgate"))
                else:
                    w_up, w_gate = W["sup"][:], W["sgate"][:]
                mm(ps[:, first + 1, :], w_up, xT[:, cols])
                mm(ps[:, first, :], w_gate, xT[:, cols]).then_inc(sem("moe1_up"), 1)
            pe.wait_ge(sem("moe1_hidden"), (CX + 1) * HALVES)
            out_tiles("moe1_result", [(hidden[:, c, :], W["xdown"][:, c, :]) for c in range(CX)]
                      + [(hidden[:, CX, :], W["sdown"][:])])


_INS = ['x', 'ctx_1024', 'mask_BxS2_bk0', 'L0_xattn_Wq', 'L0_xattn_Wkv', 'L0_xattn_Wproj', 'L0_xattn_bproj',
        'L0_ffn_Wq', 'L0_ffn_Wk', 'L0_ffn_Wv', 'L0_ffn_Wo', 'L0_ffn_g1', 'L0_ffn_b1', 'L0_ffn_g2', 'L0_ffn_b2',
        'L0_ffn_Wg', 'L0_ffn_W1', 'L0_ffn_W2', 'L1_xattn_Wq1', 'L1_xattn_Wk1', 'L1_xattn_Wv1', 'L1_xattn_bv1',
        'L1_xattn_Wq2', 'L1_xattn_Wk2', 'L1_xattn_Wv2', 'L1_xattn_bv2', 'L1_xattn_g1', 'L1_xattn_be1',
        'L1_xattn_g2', 'L1_xattn_be2', 'L1_xattn_g3', 'L1_xattn_be3', 'L1_xattn_Wf1', 'L1_xattn_bf1',
        'L1_xattn_Wf2', 'L1_xattn_bf2', 'L1_ffn_router', 'L1_ffn_experts_gate', 'L1_ffn_experts_up',
        'L1_ffn_experts_down', 'L1_ffn_shared_gate', 'L1_ffn_shared_up', 'L1_ffn_shared_down']


def kernel(**inputs):
    import numpy as _np
    import concourse.bacc as _bacc
    from concourse import mybir as _mybir
    from concourse.bass_utils import run_bass_kernel_spmd as _run

    nc = _bacc.Bacc("TRN2", target_bir_lowering=False, num_devices=1)
    arrays, io = {}, {}
    for name in _INS:
        a = _np.ascontiguousarray(inputs[name])
        arrays[f"in_{name}_dram"] = a
        io[name] = nc.dram_tensor(f"in_{name}_dram", a.shape, _mybir.dt.from_np(a.dtype), kind="ExternalInput").ap()
    out = nc.dram_tensor("out_0_dram", (1, N, D), F32, kind="ExternalOutput").ap()
    transformer(nc, io, out)
    r = _run(nc, [arrays], core_ids=[0])
    return r.results[0]["out_0_dram"]
```
